# Optimizing a Trainium2 kernel written in Bass

```python
import numpy as np
import jax
import jax.numpy as jnp

def _softmax(x, axis=-1):
    return jax.nn.softmax(x, axis=axis)

def _gelu(x):
    return jax.nn.gelu(x, approximate=True)

def _silu(x):
    return jax.nn.silu(x)

def _sigmoid(x):
    return jax.nn.sigmoid(x)

def _layernorm(x, axis=-1, eps=1e-05):
    m = jnp.mean(x, axis=axis, keepdims=True)
    v = jnp.var(x, axis=axis, keepdims=True)
    return (x - m) / jnp.sqrt(v + eps)

def _scatter_add(tgt, idx, src, axis=0):
    return tgt.at[idx].add(src)

def _segment_sum(src, seg, n):
    return jax.ops.segment_sum(src, seg, n)
kernel_name = 'mk_macaron_d1_jaxref_r8_8792a2'

def setup_inputs(seed: int=0):
    np.random.seed(seed)
    _w = jnp.asarray

    def _L0_attn_setup():
        import jax, jax.numpy as jnp
        import numpy as np
        D = 128
        B = 4
        S = 512
        LN_EPS = 1e-05

        def _layer_norm(x, gamma, beta):
            mu = jnp.mean(x, axis=-1, keepdims=True)
            var = jnp.mean(jnp.square(x - mu), axis=-1, keepdims=True)
            return (x - mu) * jax.lax.rsqrt(var + LN_EPS) * gamma + beta
        key = jax.random.key(seed)
        ks = jax.random.split(key, 5)
        scale = 1.0 / np.sqrt(D)
        return {'hidden_states': jax.random.normal(ks[0], (B, S, D), dtype=jnp.float32), 'attention_mask': jnp.ones((B, S), dtype=jnp.int32), 'Wk': jax.random.normal(ks[1], (D, D), dtype=jnp.float32) * scale, 'bk': jnp.zeros((D,), dtype=jnp.float32), 'Wka': jax.random.normal(ks[2], (D, D), dtype=jnp.float32) * scale, 'bka': jnp.zeros((D,), dtype=jnp.float32), 'Wv': jax.random.normal(ks[3], (D, D), dtype=jnp.float32) * scale, 'bv': jnp.zeros((D,), dtype=jnp.float32), 'gamma': jnp.ones((D,), dtype=jnp.float32), 'beta': jnp.zeros((D,), dtype=jnp.float32)}
    _L0_attn_in = _L0_attn_setup()

    def _L0_ffn_setup():
        import jax, jax.numpy as jnp
        import numpy as np
        import math
        BETA = 0.9
        THRESHOLD = 1.0
        NUM_STEPS = 5
        ALPHA = 2.0

        @jax.custom_vjp
        def spike_fn(u):
            return (u > 0).astype(u.dtype)

        def _spike_fwd(u):
            return (spike_fn(u), u)

        def _spike_bwd(u, g):
            s = jnp.pi / 2.0 * ALPHA * u
            return (g * (ALPHA / 2.0) / (1.0 + s * s),)
        spike_fn.defvjp(_spike_fwd, _spike_bwd)
        key = jax.random.key(seed)
        k1, k2, k3 = jax.random.split(key, 3)
        n_embd = 128
        x = jax.random.normal(k1, (4, 256, n_embd), dtype=jnp.float32)
        W_fc = jax.random.normal(k2, (4 * n_embd, n_embd), dtype=jnp.float32) / math.sqrt(n_embd)
        W_proj = jax.random.normal(k3, (n_embd, 4 * n_embd), dtype=jnp.float32) / math.sqrt(4 * n_embd)
        return {'x': x, 'W_fc': W_fc, 'W_proj': W_proj}
    _L0_ffn_in = _L0_ffn_setup()
    _d = {'L0_attn_hidden_states': _L0_attn_in['hidden_states'], 'L0_attn_attention_mask': _L0_attn_in['attention_mask'], 'L0_attn_Wk': _L0_attn_in['Wk'], 'L0_attn_bk': _L0_attn_in['bk'], 'L0_attn_Wka': _L0_attn_in['Wka'], 'L0_attn_bka': _L0_attn_in['bka'], 'L0_attn_Wv': _L0_attn_in['Wv'], 'L0_attn_bv': _L0_attn_in['bv'], 'L0_attn_gamma': _L0_attn_in['gamma'], 'L0_attn_beta': _L0_attn_in['beta'], 'L0_ffn_W_fc': _L0_ffn_in['W_fc'], 'L0_ffn_W_proj': _L0_ffn_in['W_proj']}
    _x0 = _d['L0_attn_hidden_states']
    _d['L0_attn_hidden_states'] = jax.random.normal(jax.random.fold_in(jax.random.key(seed), 1), (8, 512, 128), dtype=_x0.dtype)
    del _x0
    return _d

def reference(L0_attn_hidden_states, L0_attn_attention_mask, L0_attn_Wk, L0_attn_bk, L0_attn_Wka, L0_attn_bka, L0_attn_Wv, L0_attn_bv, L0_attn_gamma, L0_attn_beta, L0_ffn_W_fc, L0_ffn_W_proj):

    def _L0_attn_ref(hidden_states, attention_mask, Wk, bk, Wka, bka, Wv, bv, gamma, beta):
        import jax, jax.numpy as jnp
        import numpy as np
        D = 128
        B = 4
        S = 512
        LN_EPS = 1e-05

        def _layer_norm(x, gamma, beta):
            mu = jnp.mean(x, axis=-1, keepdims=True)
            var = jnp.mean(jnp.square(x - mu), axis=-1, keepdims=True)
            return (x - mu) * jax.lax.rsqrt(var + LN_EPS) * gamma + beta
        h = _layer_norm(hidden_states, gamma, beta)
        d_model = h.shape[-1]
        keys = jnp.einsum('bsd,ed->bse', h, Wk) + bk
        values = jnp.einsum('bsd,ed->bse', h, Wv) + bv
        key_att = jnp.einsum('bsd,ed->bse', keys, Wka) + bka
        keys_weight = jnp.exp(key_att / jnp.sqrt(jnp.asarray(d_model, h.dtype)))
        keys_weight = keys_weight / jnp.cumsum(keys_weight, axis=1)
        pooled_keys = jnp.cumsum(keys_weight * keys, axis=1)
        return pooled_keys * values

    def _L0_ffn_ref(x, W_fc, W_proj):
        import jax, jax.numpy as jnp
        import numpy as np
        import math
        BETA = 0.9
        THRESHOLD = 1.0
        NUM_STEPS = 5
        ALPHA = 2.0

        @jax.custom_vjp
        def spike_fn(u):
            return (u > 0).astype(u.dtype)

        def _spike_fwd(u):
            return (spike_fn(u), u)

        def _spike_bwd(u, g):
            s = jnp.pi / 2.0 * ALPHA * u
            return (g * (ALPHA / 2.0) / (1.0 + s * s),)
        spike_fn.defvjp(_spike_fwd, _spike_bwd)
        h = jnp.square(jax.nn.relu(jnp.einsum('bsd,fd->bsf', x, W_fc)))
        y = jnp.einsum('bsf,df->bsd', h, W_proj)

        def step(mem, _):
            reset = jax.lax.stop_gradient(spike_fn(mem - THRESHOLD))
            mem_new = BETA * mem + y - reset * THRESHOLD
            spk = spike_fn(mem_new - THRESHOLD)
            return (mem_new, spk)
        mem0 = jnp.zeros_like(y)
        _, spks = jax.lax.scan(step, mem0, None, length=NUM_STEPS)
        return jnp.sum(spks, axis=0) / NUM_STEPS
    x = L0_attn_hidden_states
    x = x + 0.5 * _L0_ffn_ref(_layernorm(x, axis=-1), L0_ffn_W_fc, L0_ffn_W_proj)
    x = x + _L0_attn_ref(_layernorm(x, axis=-1), L0_attn_attention_mask, L0_attn_Wk, L0_attn_bk, L0_attn_Wka, L0_attn_bka, L0_attn_Wv, L0_attn_bv, L0_attn_gamma, L0_attn_beta)
    x = x + 0.5 * _L0_ffn_ref(_layernorm(x, axis=-1), L0_ffn_W_fc, L0_ffn_W_proj)
    return x

_drawn_inputs = setup_inputs


def setup_inputs(seed=0):
    import zlib

    import numpy as np

    out = dict(_drawn_inputs(seed))
    spreads = {'L0_attn_bk': (0.0, 0.1),
     'L0_attn_bka': (0.0, 0.1),
     'L0_attn_bv': (0.0, 0.1),
     'L0_attn_gamma': (1.0, 0.2),
     'L0_attn_beta': (0.0, 0.1)}
    factors = {}
    for name, (base, spread) in spreads.items():
        noise = np.random.default_rng([zlib.crc32(name.encode()), seed]).standard_normal(out[name].shape)
        drawn = base * np.exp(spread * noise) if base else spread * noise
        out[name] = jnp.asarray(drawn.astype(out[name].dtype))
    for name, factor in factors.items():
        out[name] = (out[name] * factor).astype(out[name].dtype)
    return out
```

```python
from contextlib import ExitStack

import numpy as np

import concourse.bass as bass
from concourse import mybir

P = 128
F32 = mybir.dt.float32
F32R = mybir.dt.float32r
BF16 = mybir.dt.bfloat16
ALU = mybir.AluOpType
ACT = mybir.ActivationFunctionType

LN_EPS = 1e-5
SPIKE_DECAY, SPIKE_THRESHOLD, SPIKE_STEPS = 0.9, 1.0, 5
STAGES = ("f1", "at", "f2")
POOL_SQUARES = (2, 3)


class Batch:

    def __init__(self, pair, offset):
        self.pair = pair + offset // 2
        self.parity = offset % 2
        self.n = 2 * pair + offset

    def within(self, batches):
        return not isinstance(self.n, int) or 0 <= self.n < batches

    def after(self, k):
        return not isinstance(self.n, int) or self.n >= k


def spike_count(y):
    one = np.float32(SPIKE_THRESHOLD)
    mem, count = np.float32(0), 0
    for _ in range(SPIKE_STEPS):
        reset = np.float32(mem - one > 0)
        mem = np.float32(np.float32(np.float32(SPIKE_DECAY) * mem) + y) - reset * one
        count += int(mem - one > 0)
    return count


def spike_levels():
    levels = []
    for k in range(1, SPIKE_STEPS + 1):
        low, high = (int(np.float32(v).view(np.uint32)) for v in (0.1, 2.0))
        while high - low > 1:
            mid = (low + high) // 2
            if spike_count(np.uint32(mid).view(np.float32)) >= k:
                high = mid
            else:
                low = mid
        levels.append(np.uint32(low).view(np.float32))
    return levels


def sign_form(level):
    ulp = 2.0 ** (int(np.floor(np.log2(level))) - 23)
    middle2 = 2 * int(float(level) / ulp) + 1
    for k in range(1, 4096):
        scale = 2**23 + k
        product = scale * middle2
        bias = float(np.float32(product * ulp * 2.0**-24))
        off = abs(int(bias / ulp * 2.0**24) - product)
        if off < 2**21:
            return scale * 2.0**-23, -bias
    raise ValueError("no scale separates the two")


def macaron_kernel(nc, x, wk, bk, wka, bka, wv, bv, gamma, beta, w_fc, w_proj, out):
    NB, S, D = x.shape
    NT = S // P
    FF = w_fc.shape[0]
    NC = FF // P
    assert D == P and S == 512 and FF == 512 and NB % 2 == 0 and NB >= 8
    KEY_SCALE = float(1.0 / np.sqrt(np.float32(D)))
    LEVELS = [sign_form(level) for level in spike_levels()]
    NL = len(LEVELS)
    RESIDUAL_STEP = 0.5 / SPIKE_STEPS
    VAR_AFFINE = {"f1": (1.0, LN_EPS), "at": (1.0 + LN_EPS, LN_EPS * LN_EPS), "f2": (1.0, LN_EPS)}

    with ExitStack() as ctx:
        def sb(name, shape, dtype=F32):
            return ctx.enter_context(nc.sbuf_tensor(name, shape, dtype))

        def sem(name):
            return ctx.enter_context(nc.semaphore(name))

        def sems(name):
            return {s: sem(f"{name}_{s}") for s in STAGES}

        def bank(name):
            return ctx.enter_context(nc.psum_tensor(name, [P, 512], F32))

        hidden = {s: [bank(f"hidden_{s}_{k}") for k in range(2)] for s in ("f1", "f2")}
        work = {s: bank(f"work_{s}") for s in STAGES}
        value_ps = bank("value_ps")

        ident = sb("ident", [P, P])
        ident16 = sb("ident16", [P, P], BF16)
        ones = sb("ones", [P, S])
        ones16 = sb("ones16", [P, S], BF16)
        offset16 = sb("offset16", [P, P], BF16)
        minus_half = sb("minus_half", [P, NT])
        fc_raw = sb("fc_raw", [P, NC, P])
        proj_raw = sb("proj_raw", [P, NC, P])
        att_raw = sb("att_raw", [P, 3, P])
        vectors = sb("vectors", [P, 5])
        fc_hi = sb("fc_hi", [P, NC, P], F32R)
        fc_lo = sb("fc_lo", [P, NC, P], F32R)
        proj_t = sb("proj_t", [P, NC, P])
        att_t = sb("att_t", [P, 3, P])
        kv_full = sb("kv_full", [P, 2, P])
        kv_hi = sb("kv_hi", [P, 2, P], F32R)
        kv_lo = sb("kv_lo", [P, 2, P], F32R)
        kv_bias = sb("kv_bias", [P, 2])
        key_bias = sb("key_bias", [P, 1])

        x_in = {s: [sb(f"x_{s}_{k}", [P, NT, P]) for k in range(2)] for s in (*STAGES, "out")}
        NEXT = {"f1": "at", "at": "f2", "f2": "out"}

        stats = {s: sb(f"stats_{s}", [P, NT, 6]) for s in STAGES}
        moments = {s: sb(f"moments_{s}", [P, NT, 2]) for s in STAGES}
        neg_mean = {s: sb(f"neg_mean_{s}", [P, NT]) for s in STAGES}
        var_eps = {s: sb(f"var_eps_{s}", [P, NT]) for s in STAGES}
        rstd = {s: sb(f"rstd_{s}", [P, NT]) for s in STAGES}
        normed = {s: sb(f"normed_{s}", [P, NT, P]) for s in STAGES}
        in_hi = {s: sb(f"in_hi_{s}", [P, S], F32R) for s in STAGES}
        in_lo = {s: sb(f"in_lo_{s}", [P, S], F32R) for s in STAGES}
        relu = {s: sb(f"relu_{s}", [P, NC, S]) for s in ("f1", "f2")}
        square = {s: sb(f"square_{s}", [P, NC, S]) for s in ("f1", "f2")}
        signs = {s: sb(f"signs_{s}", [P, NL, S], BF16) for s in ("f1", "f2")}
        key = sb("key", [P, S])
        weight = sb("weight", [P, S])
        weight_sum = sb("weight_sum", [P, S])
        inv_sum = sb("inv_sum", [P, S])
        share = sb("share", [P, S])
        share_key = sb("share_key", [P, S])
        pooled = sb("pooled", [P, S])
        attended = sb("attended", [P, S])

        weights_loaded = sem("weights_loaded")
        zeros_made, ident_made = sem("zeros_made"), sem("ident_made")
        consts_made = sem("consts_made")
        ident16_made = sem("ident16_made")
        weights_turned = sem("weights_turned")
        fc_hi_made, fc_ready = sem("fc_hi_made"), sem("fc_ready")
        proj_ready = sem("proj_ready")
        att_copied = sem("att_copied")
        kv_full_made, kv_hi_made, kv_ready = sem("kv_full_made"), sem("kv_hi_made"), sem("kv_ready")
        bias_ready = sem("bias_ready")
        x_loaded = [sem(f"x_loaded_{k}") for k in range(2)]
        out_stored = [sem(f"out_stored_{k}") for k in range(2)]
        stats_made, moments_made = sems("stats_made"), sems("moments_made")
        ln_args_made, rstd_made = sems("ln_args_made"), sems("rstd_made")
        normed_made = sems("normed_made")
        turned = sems("turned")
        hi_made, lo_made = sems("hi_made"), sems("lo_made")
        hidden_made = sems("hidden_made")
        relu_made = sems("relu_made")
        squares_act, squares_pool = sems("squares_act"), sems("squares_pool")
        y_made, signs_made, count_made = sems("y_made"), sems("signs_made"), sems("count_made")
        x_updated = sems("x_updated")
        key_mm, value_mm, key_made = sem("key_mm"), sem("value_mm"), sem("key_made")
        att_mm, weight_made, sum_made = sem("att_mm"), sem("weight_made"), sem("sum_made")
        inv_made, share_made, share_key_made = sem("inv_made"), sem("share_made"), sem("share_key_made")
        pooled_made, attended_made, attended_turned = sem("pooled_made"), sem("attended_made"), sem("attended_turned")

        ACT_SQUARES = [c for c in range(NC) if c not in POOL_SQUARES]
        FIRST_STEPS = 3
        LOOP_TRIPS = (NB - 1 - FIRST_STEPS) // 2
        LAST_FROM = FIRST_STEPS + 2 * LOOP_TRIPS
        STEPS = NB + 3

        def run_steps(engine, step):
            def steps(pair, offsets):
                for o in offsets:
                    step(lambda k, o=o: Batch(pair, o - k))

            steps(0, range(FIRST_STEPS))
            for trip in range(LOOP_TRIPS):
                steps(trip, (FIRST_STEPS, FIRST_STEPS + 1))
            steps(0, range(LAST_FROM, STEPS))

        x_tiles = x.rearrange("b (t p) d -> b p t d", p=P)
        out_tiles = out.rearrange("b (t p) d -> b p t d", p=P)
        block = ctx.enter_context(nc.Block())

        @block.sync
        def _(sp):
            def load(b):
                if not b.within(NB):
                    return
                if b.after(2):
                    sp.wait_ge(x_updated["f1"], b.n - 1)
                src = x_tiles[b.n] if isinstance(b.n, int) else x_tiles[bass.ds(b.n, 1)].rearrange("b p t d -> (b p) t d")
                sp.dma_start(x_in["f1"][b.parity][:], src).then_inc(x_loaded[b.parity], 16)

            def store(b):
                if not b.within(NB):
                    return
                sp.wait_ge(x_updated["f2"], b.n + 1)
                dst = out_tiles[b.n] if isinstance(b.n, int) else out_tiles[bass.ds(b.n, 1)].rearrange("b p t d -> (b p) t d")
                sp.dma_start(dst, x_in["out"][b.parity][:]).then_inc(out_stored[b.parity], 16)

            load(Batch(0, 0))
            sp.dma_start(fc_raw[:], w_fc.rearrange("(c p) d -> p c d", p=P)).then_inc(weights_loaded, 16)

            def step(at):
                load(at(-1))
                store(at(3))

            run_steps(sp, step)
            for k in range(2):
                sp.wait_ge(out_stored[k], 16 * (NB // 2))

        @block.gpsimd
        def _(pool):
            nc.gpsimd.memset(minus_half[:], -0.5).then_inc(zeros_made, 1)
            nc.gpsimd.memset(ident[:], 0.0).then_inc(zeros_made, 1)
            pool.wait_ge(zeros_made, 2)
            nc.gpsimd.affine_select(out=ident[:], in_=ident[:], compare_op=ALU.not_equal, fill=1.0,
                                    base=0, pattern=[[-1, P]], channel_multiplier=1).then_inc(ident_made, 1)

            def normalise(s, b):
                if not b.within(NB):
                    return
                pool.wait_ge(ln_args_made[s], 2 * (b.n + 1))
                nc.gpsimd.tensor_tensor(rstd[s][:], var_eps[s][:], minus_half[:], ALU.pow).then_inc(rstd_made[s], 1)
                pool.wait_ge(rstd_made[s], b.n + 1)
                if b.after(1):
                    pool.wait_ge(turned[s], b.n)
                for t in range(NT):
                    nc.gpsimd.tensor_scalar(normed[s][:, t, :], x_in[s][b.parity][:, t, :],
                                            neg_mean[s][:, t:t + 1], rstd[s][:, t:t + 1],
                                            ALU.add, ALU.mult).then_inc(normed_made[s], 1)

            def squares(s, b):
                if not b.within(NB):
                    return
                for c in POOL_SQUARES:
                    pool.wait_ge(relu_made[s], NC * b.n + c + 1)
                    nc.gpsimd.tensor_tensor(square[s][:, c, :], relu[s][:, c, :], relu[s][:, c, :],
                                            ALU.mult).then_inc(squares_pool[s], 1)

            def shares(b):
                if not b.within(NB):
                    return
                pool.wait_ge(inv_made, b.n + 1)
                nc.gpsimd.tensor_tensor(share[:], weight[:], inv_sum[:], ALU.mult).then_inc(share_made, 1)
                pool.wait_ge(share_made, b.n + 1)
                nc.gpsimd.tensor_tensor(share_key[:], share[:], key[:], ALU.mult).then_inc(share_key_made, 1)

            normalise("f1", Batch(0, 0))

            def step(at):
                normalise("at", at(1))
                normalise("f2", at(2))
                squares("f1", at(0))
                normalise("f1", at(-1))
                shares(at(1))
                squares("f2", at(2))

            run_steps(pool, step)

        @block.scalar
        def _(act):
            act.dma_start(att_raw[:, 0, :], wk).then_inc(weights_loaded, 16)
            act.dma_start(att_raw[:, 1, :], wv).then_inc(weights_loaded, 16)
            act.dma_start(att_raw[:, 2, :], wka).then_inc(weights_loaded, 16)
            act.dma_start(proj_raw[:], w_proj.rearrange("d (c f) -> d c f", f=P)).then_inc(weights_loaded, 16)
            for k, v in enumerate((bk, bv, bka, gamma, beta)):
                act.dma_start(vectors[:, k:k + 1], v.rearrange("(p a) -> p a", a=1)).then_inc(weights_loaded, 16)

            def part_hi(s, b):
                if not b.within(NB):
                    return
                act.wait_ge(turned[s], b.n + 1)
                nc.scalar.activation(in_hi[s][:], work[s][:], ACT.Copy).then_inc(hi_made[s], 1)

            def rectify(s, b, c):
                if not b.within(NB):
                    return
                act.wait_ge(hidden_made[s], NC * b.n + c + 1)
                nc.scalar.activation(relu[s][:, c, :], hidden[s][c % 2][:], ACT.Relu).then_inc(relu_made[s], 1)

            def squares(s, b):
                if not b.within(NB):
                    return
                for c in ACT_SQUARES:
                    act.wait_ge(relu_made[s], NC * b.n + c + 1)
                    nc.scalar.activation(square[s][:, c, :], relu[s][:, c, :], ACT.Square).then_inc(squares_act[s], 1)

            def compare(s, b, levels):
                if not b.within(NB):
                    return
                for k in levels:
                    if k == 0:
                        act.wait_ge(y_made[s], b.n + 1)
                    scale, bias = LEVELS[k]
                    nc.scalar.activation(signs[s][:, k, :], work[s][:], ACT.Sign, bias=bias,
                                         scale=scale).then_inc(signs_made[s], 1)

            def key_out(b):
                if not b.within(NB):
                    return
                act.wait_ge(key_mm, b.n + 1)
                if not b.after(1):
                    act.wait_ge(bias_ready, 2)
                nc.scalar.activation(key[:], work["at"][:], ACT.Identity, bias=kv_bias[:, 0:1]).then_inc(key_made, 1)

            def exponent(b):
                if not b.within(NB):
                    return
                act.wait_ge(att_mm, b.n + 1)
                nc.scalar.activation(weight[:], work["at"][:], ACT.Exp, bias=key_bias[:, 0:1],
                                     scale=KEY_SCALE).then_inc(weight_made, 1)

            act.wait_ge(weights_turned, 1)
            nc.scalar.activation(fc_hi[:].rearrange("p c f -> p (c f)"), hidden["f2"][0][:], ACT.Copy).then_inc(fc_hi_made, 1)
            act.wait_ge(weights_turned, 2)
            nc.scalar.activation(proj_t[:].rearrange("p c f -> p (c f)"), hidden["f2"][1][:], ACT.Copy).then_inc(proj_ready, 1)
            part_hi("f1", Batch(0, 0))

            def step(at):
                compare("f2", at(3), (0,))
                rectify("f1", at(0), 0)
                compare("f2", at(3), (1,))
                rectify("f1", at(0), 1)
                compare("f2", at(3), (2,))
                part_hi("at", at(1))
                compare("f2", at(3), (3,))
                rectify("f1", at(0), 2)
                compare("f2", at(3), (4,))
                rectify("f1", at(0), 3)
                key_out(at(1))
                squares("f1", at(0))
                part_hi("f2", at(2))
                exponent(at(1))
                rectify("f2", at(2), 0)
                rectify("f2", at(2), 1)
                squares("f2", at(2))
                compare("f1", at(0), (0, 1, 2))
                rectify("f2", at(2), 2)
                compare("f1", at(0), (3, 4))
                rectify("f2", at(2), 3)
                part_hi("f1", at(-1))

            run_steps(act, step)

        @block.vector
        def _(dve):
            def ln_stats(s, b):
                if not b.within(NB):
                    return
                if s == "f1":
                    dve.wait_ge(x_loaded[b.parity], 16 * (b.pair + 1))
                else:
                    dve.wait_ge(x_updated["f1" if s == "at" else "at"], b.n + 1)
                for t in range(NT):
                    nc.vector.bn_stats(stats[s][:, t, :], x_in[s][b.parity][:, t, :]).then_inc(stats_made[s], 1)

            def ln_args(s, b):
                if not b.within(NB):
                    return
                for t in range(NT):
                    dve.wait_ge(stats_made[s], NT * b.n + t + 1)
                    nc.vector.bn_aggr(moments[s][:, t, :], stats[s][:, t, :]).then_inc(moments_made[s], 1)
                if b.after(1):
                    dve.wait_ge(normed_made[s], NT * b.n)
                dve.wait_ge(moments_made[s], NT * (b.n + 1))
                a, c = VAR_AFFINE[s]
                nc.vector.tensor_scalar(var_eps[s][:], moments[s][:, :, 1], a, c, ALU.mult, ALU.add).then_inc(ln_args_made[s], 1)
                nc.vector.tensor_scalar(neg_mean[s][:], moments[s][:, :, 0], -1.0, None, ALU.mult).then_inc(ln_args_made[s], 1)

            def part_lo(s, b):
                if not b.within(NB):
                    return
                dve.wait_ge(hi_made[s], b.n + 1)
                nc.vector.tensor_tensor(in_lo[s][:], work[s][:], in_hi[s][:].bitcast(F32), ALU.subtract).then_inc(lo_made[s], 1)

            def add_spikes(s, b):
                if not b.within(NB):
                    return
                dve.wait_ge(count_made[s], b.n + 1)
                if s == "f2" and b.after(2):
                    dve.wait_ge(out_stored[b.parity], 16 * b.pair)
                nc.vector.scalar_tensor_tensor(
                    x_in[NEXT[s]][b.parity][:].rearrange("p t d -> p (t d)"), work[s][:], RESIDUAL_STEP / 2,
                    x_in[s][b.parity][:].rearrange("p t d -> p (t d)"), ALU.mult, ALU.add).then_inc(x_updated[s], 1)

            def running_sum(b):
                if not b.within(NB):
                    return
                dve.wait_ge(weight_made, b.n + 1)
                nc.vector.tensor_tensor_scan(weight_sum[:], ones[:], weight[:], 0.0, ALU.mult, ALU.add).then_inc(sum_made, 1)
                dve.wait_ge(sum_made, b.n + 1)
                nc.vector.reciprocal(inv_sum[:], weight_sum[:]).then_inc(inv_made, 1)

            def pool_keys(b):
                if not b.within(NB):
                    return
                dve.wait_ge(share_key_made, b.n + 1)
                nc.vector.tensor_tensor_scan(pooled[:], ones[:], share_key[:], 0.0, ALU.mult, ALU.add).then_inc(pooled_made, 1)
                dve.wait_ge(pooled_made, b.n + 1)
                dve.wait_ge(value_mm, b.n + 1)
                nc.vector.scalar_tensor_tensor(attended[:], value_ps[:], kv_bias[:, 1:2], pooled[:],
                                               ALU.add, ALU.mult).then_inc(attended_made, 1)

            def add_attention(b):
                if not b.within(NB):
                    return
                dve.wait_ge(attended_turned, b.n + 1)
                nc.vector.tensor_tensor(x_in["f2"][b.parity][:].rearrange("p t d -> p (t d)"), work["at"][:],
                                        x_in["at"][b.parity][:].rearrange("p t d -> p (t d)"),
                                        ALU.add).then_inc(x_updated["at"], 1)

            nc.vector.memset(ones[:], 1.0).then_inc(consts_made, 1)
            nc.vector.memset(ones16[:], 1.0).then_inc(consts_made, 1)
            nc.vector.memset(offset16[:], NL / P).then_inc(consts_made, 1)
            ln_stats("f1", Batch(0, 0))
            ln_args("f1", Batch(0, 0))
            dve.wait_ge(ident_made, 1)
            nc.vector.tensor_copy(ident16[:], ident[:]).then_inc(ident16_made, 1)
            dve.wait_ge(fc_hi_made, 1)
            nc.vector.tensor_tensor(fc_lo[:].rearrange("p c f -> p (c f)"), hidden["f2"][0][:],
                                    fc_hi[:].bitcast(F32).rearrange("p c f -> p (c f)"), ALU.subtract).then_inc(fc_ready, 1)
            part_lo("f1", Batch(0, 0))
            dve.wait_ge(weights_turned, 3)
            nc.vector.tensor_copy(att_t[:].rearrange("p a f -> p (a f)"), work["f2"][:, 0:3 * P]).then_inc(att_copied, 1)
            dve.wait_ge(att_copied, 1)
            nc.vector.tensor_scalar(kv_full[:], att_t[:, 0:2, :], vectors[:, 3:4], None, ALU.mult).then_inc(kv_full_made, 1)
            dve.wait_ge(kv_full_made, 1)
            nc.vector.tensor_copy(kv_hi[:], kv_full[:]).then_inc(kv_hi_made, 1)
            dve.wait_ge(kv_hi_made, 1)
            nc.vector.tensor_tensor(kv_lo[:], kv_full[:], kv_hi[:].bitcast(F32), ALU.subtract).then_inc(kv_ready, 1)
            dve.wait_ge(weights_turned, 4)
            nc.vector.tensor_tensor(kv_bias[:], work["at"][:, 0:2], vectors[:, 0:2], ALU.add).then_inc(bias_ready, 1)
            nc.vector.tensor_scalar(key_bias[:], vectors[:, 2:3], KEY_SCALE, None, ALU.mult).then_inc(bias_ready, 1)

            def step(at):
                ln_stats("f2", at(2))
                ln_args("f2", at(2))
                part_lo("at", at(1))
                add_spikes("f2", at(3))
                ln_stats("f1", at(-1))
                ln_args("f1", at(-1))
                part_lo("f2", at(2))
                running_sum(at(1))
                pool_keys(at(1))
                add_spikes("f1", at(0))
                ln_stats("at", at(0))
                part_lo("f1", at(-1))
                ln_args("at", at(0))
                add_attention(at(1))

            run_steps(dve, step)

        @block.tensor
        def _(pe):
            def turn_in(s, b):
                if not b.within(NB):
                    return
                if b.after(1):
                    pe.wait_ge(x_updated[s], b.n)
                for t in range(NT):
                    pe.wait_ge(normed_made[s], NT * b.n + t + 1)
                    last = nc.tensor.transpose(work[s][:, t * P:(t + 1) * P], normed[s][:, t, :], ident[:])
                last.then_inc(turned[s], 1)

            def product(dst, w_hi, w_lo, s):
                nc.tensor.matmul(dst, w_lo, in_hi[s][:], start=True, stop=False)
                nc.tensor.matmul(dst, w_hi, in_lo[s][:], start=False, stop=False)
                return nc.tensor.matmul(dst, w_hi, in_hi[s][:], start=False, stop=True)

            def expand(s, b, chunks):
                if not b.within(NB):
                    return
                for c in chunks:
                    if c == 0:
                        pe.wait_ge(lo_made[s], b.n + 1)
                    if c >= 2 or b.after(1):
                        pe.wait_ge(relu_made[s], NC * b.n + c - 1)
                    product(hidden[s][c % 2][:], fc_hi[:, c, :], fc_lo[:, c, :], s).then_inc(hidden_made[s], 1)

            def contract(s, b, chunks):
                if not b.within(NB):
                    return
                for c in chunks:
                    if c in ACT_SQUARES:
                        pe.wait_ge(squares_act[s], len(ACT_SQUARES) * b.n + ACT_SQUARES.index(c) + 1)
                    else:
                        pe.wait_ge(squares_pool[s], len(POOL_SQUARES) * b.n + POOL_SQUARES.index(c) + 1)
                    last = nc.tensor.matmul(work[s][:], proj_t[:, c, :], square[s][:, c, :],
                                            start=(c == 0), stop=(c == NC - 1))
                    if c == NC - 1:
                        last.then_inc(y_made[s], 1)

            def count_spikes(s, b):
                if not b.within(NB):
                    return
                pe.wait_ge(signs_made[s], NL * (b.n + 1))
                nc.tensor.matmul(work[s][:], offset16[:], ones16[:], start=True, stop=False, skip_group_check=True)
                for t in range(NT):
                    for k in range(NL):
                        last = nc.tensor.matmul(work[s][:, t * P:(t + 1) * P], signs[s][:, k, t * P:(t + 1) * P],
                                                ident16[:], start=False, stop=(k == NL - 1), skip_group_check=True)
                last.then_inc(count_made[s], 1)

            def keys_values(b):
                if not b.within(NB):
                    return
                pe.wait_ge(lo_made["at"], b.n + 1)
                product(work["at"][:], kv_hi[:, 0, :], kv_lo[:, 0, :], "at").then_inc(key_mm, 1)
                product(value_ps[:], kv_hi[:, 1, :], kv_lo[:, 1, :], "at").then_inc(value_mm, 1)

            def key_attention(b):
                if not b.within(NB):
                    return
                pe.wait_ge(key_made, b.n + 1)
                nc.tensor.matmul(work["at"][:], att_t[:, 2, :], key[:], start=True, stop=True).then_inc(att_mm, 1)

            def turn_out(b):
                if not b.within(NB):
                    return
                pe.wait_ge(attended_made, b.n + 1)
                for t in range(NT):
                    last = nc.tensor.transpose(work["at"][:, t * P:(t + 1) * P], attended[:, t * P:(t + 1) * P], ident[:])
                last.then_inc(attended_turned, 1)

            pe.wait_ge(ident_made, 1)
            pe.wait_ge(consts_made, 3)
            pe.wait_ge(weights_loaded, 16 * 10)
            for c in range(NC):
                last = nc.tensor.transpose(hidden["f2"][0][:, c * P:(c + 1) * P], fc_raw[:, c, :], ident[:])
            last.then_inc(weights_turned, 1)
            for c in range(NC):
                last = nc.tensor.transpose(hidden["f2"][1][:, c * P:(c + 1) * P], proj_raw[:, c, :], ident[:])
            last.then_inc(weights_turned, 1)
            turn_in("f1", Batch(0, 0))
            for a in range(3):
                last = nc.tensor.transpose(work["f2"][:, a * P:(a + 1) * P], att_raw[:, a, :], ident[:])
            last.then_inc(weights_turned, 1)
            pe.wait_ge(att_copied, 1)
            for a in range(2):
                last = nc.tensor.matmul(work["at"][:, a:a + 1], att_t[:, a, :], vectors[:, 4:5], start=True, stop=True)
            last.then_inc(weights_turned, 1)
            pe.wait_ge(fc_ready, 1)
            pe.wait_ge(proj_ready, 1)
            pe.wait_ge(kv_ready, 1)
            pe.wait_ge(ident16_made, 1)
            pe.wait_ge(bias_ready, 2)

            def step(at):
                expand("f1", at(0), (0, 1))
                turn_in("at", at(1))
                expand("f1", at(0), (2, 3))
                count_spikes("f2", at(3))
                keys_values(at(1))
                turn_in("f2", at(2))
                key_attention(at(1))
                contract("f1", at(0), (0, 1))
                expand("f2", at(2), (0, 1))
                contract("f1", at(0), (2, 3))
                expand("f2", at(2), (2, 3))
                contract("f2", at(2), (0, 1))
                count_spikes("f1", at(0))
                contract("f2", at(2), (2,))
                turn_in("f1", at(-1))
                turn_out(at(1))
                contract("f2", at(2), (3,))

            run_steps(pe, step)


_INS = ["L0_attn_hidden_states", "L0_attn_Wk", "L0_attn_bk", "L0_attn_Wka", "L0_attn_bka", "L0_attn_Wv",
        "L0_attn_bv", "L0_attn_gamma", "L0_attn_beta", "L0_ffn_W_fc", "L0_ffn_W_proj"]


def kernel(**inputs):
    import numpy as _np
    import concourse.bacc as _bacc
    from concourse import mybir as _mybir
    from concourse.bass_utils import run_bass_kernel_spmd as _run

    nc = _bacc.Bacc("TRN2", target_bir_lowering=False, num_devices=1)
    arrays, args = {}, []
    for name in _INS:
        a = _np.ascontiguousarray(inputs[name])
        arrays[f"in_{name}_dram"] = a
        args.append(nc.dram_tensor(f"in_{name}_dram", a.shape, _mybir.dt.from_np(a.dtype), kind="ExternalInput").ap())
    shape = inputs["L0_attn_hidden_states"].shape
    out = nc.dram_tensor("out_0_dram", shape, _mybir.dt.float32, kind="ExternalOutput").ap()
    macaron_kernel(nc, *args, out)
    r = _run(nc, [arrays], core_ids=[0])
    return r.results[0]["out_0_dram"]
```

```python
from contextlib import ExitStack

import numpy as np

import concourse.bass as bass
from concourse import mybir

P = 128
F32 = mybir.dt.float32
F32R = mybir.dt.float32r
BF16 = mybir.dt.bfloat16
ALU = mybir.AluOpType
ACT = mybir.ActivationFunctionType

LN_EPS = 1e-5
SPIKE_DECAY, SPIKE_THRESHOLD, SPIKE_STEPS = 0.9, 1.0, 5


FF_JOBS = [("first", b) for b in range(0, 8)] + \
          [("second", b) for b in range(0, 8)]
ATT_STEP = [3, 4, 5, 6, 8, 9, 10, 11]
CONTRACT_ORDER = (1, 0, 2, 3)
POOL_SQUARES = [(0,), (0,)]
ATT_SETS = 3
SIGN_ADDS = [4, 1]


class FeedForward:

    def __init__(self, i):
        self.layer, self.batch = FF_JOBS[i]
        self.index, self.lane, self.turn = i, i % 2, i // 2
        self.pool_squares = POOL_SQUARES[i in ATT_STEP]
        self.act_squares = [c for c in CONTRACT_ORDER if c not in self.pool_squares]
        self.sign_adds = SPIKE_STEPS - 1 if i == len(FF_JOBS) - 1 else SIGN_ADDS[i in ATT_STEP]

    def before(self, amount):
        return sum(amount(FeedForward(k)) for k in range(self.lane, self.index, 2))


def feed_forward(i):
    return [FeedForward(i)] if 0 <= i < len(FF_JOBS) else []


def attention(i):
    return [ATT_STEP.index(i)] if i in ATT_STEP else []


def spike_count(y):
    one = np.float32(SPIKE_THRESHOLD)
    mem, count = np.float32(0), 0
    for _ in range(SPIKE_STEPS):
        reset = np.float32(mem - one > 0)
        mem = np.float32(np.float32(np.float32(SPIKE_DECAY) * mem) + y) - reset * one
        count += int(mem - one > 0)
    return count


def spike_levels():
    levels = []
    for k in range(1, SPIKE_STEPS + 1):
        low, high = (int(np.float32(v).view(np.uint32)) for v in (0.1, 2.0))
        while high - low > 1:
            mid = (low + high) // 2
            if spike_count(np.uint32(mid).view(np.float32)) >= k:
                high = mid
            else:
                low = mid
        levels.append(np.uint32(low).view(np.float32))
    return levels


def sign_form(level):
    ulp = 2.0 ** (int(np.floor(np.log2(level))) - 23)
    middle2 = 2 * int(float(level) / ulp) + 1
    for k in range(1, 4096):
        scale = 2**23 + k
        product = scale * middle2
        bias = float(np.float32(product * ulp * 2.0**-24))
        off = abs(int(bias / ulp * 2.0**24) - product)
        if off < 2**21:
            return scale * 2.0**-23, -bias
    raise ValueError("no scale separates the two")


def macaron_kernel(nc, x, wk, bk, wka, bka, wv, bv, gamma, beta, w_fc, w_proj, out):
    NB, S, D = x.shape
    NT = S // P
    FF = w_fc.shape[0]
    NC = FF // P
    HALF = S // 2
    assert D == P and S == 512 and FF == 512
    assert sorted(FF_JOBS) == sorted((l, b) for l in ("first", "second") for b in range(NB))
    for b in range(NB):
        assert FF_JOBS.index(("first", b)) + 3 <= ATT_STEP[b] <= FF_JOBS.index(("second", b)) - 3
    KEY_SCALE = float(1.0 / np.sqrt(np.float32(D)))
    LEVELS = [sign_form(level) for level in spike_levels()]
    NL = len(LEVELS)
    RESIDUAL_STEP = 0.5 / SPIKE_STEPS
    OFFSET = NL * RESIDUAL_STEP / 2
    WARM_UP = 14
    STEPS = len(FF_JOBS) + 3
    FIRST_STEP = -3
    FF_AFFINE, ATT_AFFINE = (1.0, LN_EPS), (1.0 + LN_EPS, LN_EPS * LN_EPS)

    with ExitStack() as ctx:
        def sb(name, shape, dtype=F32):
            return ctx.enter_context(nc.sbuf_tensor(name, shape, dtype))

        def sem(name):
            return ctx.enter_context(nc.semaphore(name))

        def bank(name):
            return ctx.enter_context(nc.psum_tensor(name, [P, 512], F32))

        LANES = (0, 1)
        KINDS = (0, 1, "att")

        hidden = [bank(f"hidden{c}") for c in range(NC)]
        count_bank = hidden[NC - 1]
        work = [bank(f"work{l}") for l in LANES]
        att_work, att_value = bank("att_work"), bank("att_value")

        ident = sb("ident", [P, P])
        ident16 = sb("ident16", [P, P], BF16)
        ones = sb("ones", [P, S])
        minus_half = sb("minus_half", [P, NT])
        fc_raw = sb("fc_raw", [P, NC, P])
        proj_raw = sb("proj_raw", [P, NC, P])
        att_raw = sb("att_raw", [P, 3, P])
        vectors = sb("vectors", [P, 5])
        fc_hi = sb("fc_hi", [P, NC, P], F32R)
        fc_lo = sb("fc_lo", [P, NC, P], F32R)
        proj_t = sb("proj_t", [P, NC, P])
        att_t = sb("att_t", [P, 3, P])
        kv_full = sb("kv_full", [P, 2, P])
        kv_hi = sb("kv_hi", [P, 2, P], F32R)
        kv_lo = sb("kv_lo", [P, 2, P], F32R)
        kv_bias = sb("kv_bias", [P, 2])
        key_bias = sb("key_bias", [P, 1])

        x_of = {k: [sb(f"x_{k}_{b}", [P, NT, P]) for b in range(NB)] for k in ("first", "att", "second", "out")}
        NEXT = {"first": "att", "second": "out"}

        stats = {k: sb(f"stats_{k}", [P, NT, 6]) for k in KINDS}
        moments = {k: sb(f"moments_{k}", [P, NT, 2]) for k in KINDS}
        neg_mean = {k: sb(f"neg_mean_{k}", [P, NT]) for k in KINDS}
        var_eps = {k: sb(f"var_eps_{k}", [P, NT]) for k in KINDS}
        rstd = {k: sb(f"rstd_{k}", [P, NT]) for k in KINDS}
        normed = {k: sb(f"normed_{k}", [P, NT, P]) for k in KINDS}
        in_hi = [sb(f"in_hi{l}", [P, S], F32R) for l in LANES]
        in_lo = [sb(f"in_lo{l}", [P, S], F32R) for l in LANES]
        relu = [sb(f"relu{l}", [P, NC, S]) for l in LANES]
        square = [sb(f"square{l}", [P, NC, S]) for l in LANES]
        signs = [sb(f"signs{l}", [P, NL, S], BF16) for l in LANES]
        sign_sum = [sb(f"sign_sum{l}", [P, S], BF16) for l in LANES]
        att_hi = [sb(f"att_hi{k}", [P, S], F32R) for k in range(ATT_SETS)]
        att_lo = [sb(f"att_lo{k}", [P, S], F32R) for k in range(ATT_SETS)]
        key = [sb(f"key{k}", [P, S]) for k in range(ATT_SETS)]
        weight = [sb(f"weight{k}", [P, S]) for k in range(ATT_SETS)]
        weight_sum = [sb(f"weight_sum{k}", [P, S]) for k in range(ATT_SETS)]
        inv_sum = sb("inv_sum", [P, S])
        share = sb("share", [P, S])
        share_key = sb("share_key", [P, S])
        pooled = sb("pooled", [P, S])
        attended = sb("attended", [P, S])

        zeros_made, ident_made, ident16_made = sem("zeros_made"), sem("ident_made"), sem("ident16_made")
        consts_made = sem("consts_made")
        x_loaded = [sem(f"x_loaded{b}") for b in range(NB)]
        fc_loaded, proj_loaded, att_loaded = sem("fc_loaded"), sem("proj_loaded"), sem("att_loaded")
        vectors_loaded = sem("vectors_loaded")
        fc_turned, proj_turned, att_turned, beta_mm = (sem(n) for n in ("fc_turned", "proj_turned", "att_turned", "beta_mm"))
        fc_hi_made, fc_ready, proj_ready = sem("fc_hi_made"), sem("fc_ready"), sem("proj_ready")
        att_copied, kv_full_made = sem("att_copied"), sem("kv_full_made")
        kv_hi_made, kv_ready, bias_ready = sem("kv_hi_made"), sem("kv_ready"), sem("bias_ready")
        out_stored = sem("out_stored")

        def sems(name, kinds):
            return {k: sem(f"{name}_{k}") for k in kinds}

        stats_made, moments_made = sems("stats_made", KINDS), sems("moments_made", KINDS)
        ln_args_made, rstd_made = sems("ln_args_made", KINDS), sems("rstd_made", KINDS)
        normed_made = sems("normed_made", KINDS)
        turned, hi_made, lo_made = sems("turned", KINDS), sems("hi_made", KINDS), sems("lo_made", KINDS)
        hidden_made, relu_made = sems("hidden_made", LANES), sems("relu_made", LANES)
        squares_act, squares_pool = sems("squares_act", LANES), sems("squares_pool", LANES)
        y_made, count_made = sems("y_made", LANES), sems("count_made", LANES)
        signs_made = sems("signs_made", LANES)
        sign_sum_made = sems("sign_sum_made", LANES)
        x_made = sems("x_made", ("att", "second", "out"))
        key_mm, value_mm, key_made, att_mm = sem("key_mm"), sem("value_mm"), sem("key_made"), sem("att_mm")
        weight_made, sum_made, inv_made = sem("weight_made"), sem("sum_made"), sem("inv_made")
        share_made, share_key_made = sem("share_made"), sem("share_key_made")
        pooled_made, attended_made, attended_turned = sem("pooled_made"), sem("attended_made"), sem("attended_turned")

        def flat(tile):
            return tile[:].rearrange("p t d -> p (t d)")

        x_tiles = x.rearrange("b (t p) d -> b p t d", p=P)
        out_tiles = out.rearrange("b (t p) d -> b p t d", p=P)
        block = ctx.enter_context(nc.Block())

        @block.sync
        def _(sp):
            sp.dma_start(x_of["first"][0][:], x_tiles[0]).then_inc(x_loaded[0], 16)
            sp.dma_start(proj_raw[:], w_proj.rearrange("d (c f) -> d c f", f=P)).then_inc(proj_loaded, 16)
            sp.dma_start(x_of["first"][1][:], x_tiles[1]).then_inc(x_loaded[1], 16)
            for k, w in enumerate((wk, wv, wka)):
                sp.dma_start(att_raw[:, k, :], w).then_inc(att_loaded, 16)
            sp.dma_start(x_of["first"][2][:], x_tiles[2]).then_inc(x_loaded[2], 16)
            for k, v in enumerate((bk, bv, bka, gamma, beta)):
                sp.dma_start(vectors[:, k:k + 1], v.rearrange("(p a) -> p a", a=1)).then_inc(vectors_loaded, 16)
            for b in range(3, NB):
                sp.dma_start(x_of["first"][b][:], x_tiles[b]).then_inc(x_loaded[b], 16)
            for b in range(NB):
                sp.wait_ge(x_made["out"], b + 1)
                sp.dma_start(out_tiles[b], x_of["out"][b][:]).then_inc(out_stored, 16)
            sp.wait_ge(out_stored, 16 * NB)

        @block.gpsimd
        def _(pool):
            nc.gpsimd.memset(ident[:], 0.0).then_inc(zeros_made, 1)
            nc.gpsimd.memset(minus_half[:], -0.5).then_inc(zeros_made, 1)
            pool.wait_ge(zeros_made, 2)
            nc.gpsimd.affine_select(out=ident[:], in_=ident[:], compare_op=ALU.not_equal, fill=1.0,
                                    base=0, pattern=[[-1, P]], channel_multiplier=1).then_inc(ident_made, 1)

            def normalise(kind, turn, source):
                pool.wait_ge(ln_args_made[kind], 2 * (turn + 1))
                nc.gpsimd.tensor_tensor(rstd[kind][:], var_eps[kind][:], minus_half[:], ALU.pow).then_inc(rstd_made[kind], 1)
                pool.wait_ge(rstd_made[kind], turn + 1)
                if turn:
                    pool.wait_ge(turned[kind], turn)
                for t in range(NT):
                    nc.gpsimd.tensor_scalar(normed[kind][:, t, :], source[:, t, :], neg_mean[kind][:, t:t + 1],
                                            rstd[kind][:, t:t + 1], ALU.add, ALU.mult).then_inc(normed_made[kind], 1)

            def ff_normalise(j):
                normalise(j.lane, j.turn, x_of[j.layer][j.batch])

            def att_normalise(b):
                normalise("att", b, x_of["att"][b])

            def ff_squares(j):
                for n, c in enumerate(j.pool_squares):
                    pool.wait_ge(relu_made[j.lane], NC * j.turn + c + 1)
                    nc.gpsimd.tensor_tensor(square[j.lane][:, c, :], relu[j.lane][:, c, :], relu[j.lane][:, c, :],
                                            ALU.mult).then_inc(squares_pool[j.lane], 1)

            def att_shares(b, half):
                cols = slice(half * HALF, (half + 1) * HALF)
                pool.wait_ge(inv_made, 2 * b + half + 1)
                nc.gpsimd.tensor_tensor(share[:, cols], weight[b % ATT_SETS][:, cols], inv_sum[:, cols], ALU.mult).then_inc(share_made, 1)
                pool.wait_ge(share_made, 2 * b + half + 1)
                nc.gpsimd.tensor_tensor(share_key[:, cols], share[:, cols], key[b % ATT_SETS][:, cols],
                                        ALU.mult).then_inc(share_key_made, 1)

            for i in range(FIRST_STEP, STEPS):
                for b in attention(i + 1):
                    att_normalise(b)
                for b in attention(i - 1):
                    att_shares(b, 0)
                    att_shares(b, 1)
                for j in feed_forward(i + 2):
                    ff_normalise(j)
                for j in feed_forward(i + 1):
                    ff_squares(j)

        @block.scalar
        def _(act):
            act.dma_start(fc_raw[:], w_fc.rearrange("(c p) d -> p c d", p=P)).then_inc(fc_loaded, 16)

            def ff_hi(j):
                act.wait_ge(turned[j.lane], j.turn + 1)
                nc.scalar.activation(in_hi[j.lane][:], work[j.lane][:], ACT.Copy).then_inc(hi_made[j.lane], 1)

            def ff_relu(j, c):
                act.wait_ge(hidden_made[j.lane], NC * j.turn + c + 1)
                nc.scalar.activation(relu[j.lane][:, c, :], hidden[c][:], ACT.Relu).then_inc(relu_made[j.lane], 1)

            def ff_square(j, c):
                if c in j.act_squares:
                    act.wait_ge(relu_made[j.lane], NC * j.turn + c + 1)
                    nc.scalar.activation(square[j.lane][:, c, :], relu[j.lane][:, c, :],
                                         ACT.Square).then_inc(squares_act[j.lane], 1)

            def ff_sign(j, k):
                if k == 0:
                    act.wait_ge(y_made[j.lane], j.turn + 1)
                if k == 0 and j.turn:
                    act.wait_ge(count_made[j.lane], j.turn)
                scale, bias = LEVELS[k]
                nc.scalar.activation(signs[j.lane][:, k, :], work[j.lane][:], ACT.Sign, bias=bias,
                                     scale=scale).then_inc(signs_made[j.lane], 1)

            def att_part_hi(b):
                act.wait_ge(turned["att"], b + 1)
                if b >= ATT_SETS:
                    act.wait_ge(value_mm, b - ATT_SETS + 1)
                nc.scalar.activation(att_hi[b % ATT_SETS][:], att_work[:], ACT.Copy).then_inc(hi_made["att"], 1)

            def att_key(b):
                act.wait_ge(key_mm, b + 1)
                if b == 0:
                    act.wait_ge(bias_ready, 2)
                if b >= ATT_SETS:
                    act.wait_ge(share_key_made, 2 * (b - ATT_SETS + 1))
                nc.scalar.activation(key[b % ATT_SETS][:], att_work[:], ACT.Identity, bias=kv_bias[:, 0:1]).then_inc(key_made, 1)

            def att_weight(b):
                act.wait_ge(att_mm, b + 1)
                nc.scalar.activation(weight[b % ATT_SETS][:], att_work[:], ACT.Exp, bias=key_bias[:, 0:1],
                                     scale=KEY_SCALE).then_inc(weight_made, 1)

            act.wait_ge(fc_turned, 1)
            nc.scalar.activation(flat(fc_hi), hidden[2][:], ACT.Copy).then_inc(fc_hi_made, 1)
            act.wait_ge(proj_turned, 1)
            nc.scalar.activation(flat(proj_t), att_value[:], ACT.Copy).then_inc(proj_ready, 1)
            for i in range(FIRST_STEP, STEPS):
                for j in feed_forward(i - 1):
                    ff_sign(j, 0)
                    ff_sign(j, 1)
                for j in feed_forward(i):
                    ff_relu(j, 0)
                for j in feed_forward(i - 1):
                    ff_sign(j, 2)
                for j in feed_forward(i):
                    ff_relu(j, 1)
                    ff_square(j, 1)
                for j in feed_forward(i - 1):
                    ff_sign(j, 3)
                for b in attention(i):
                    att_key(b)
                for j in feed_forward(i - 1):
                    ff_sign(j, 4)
                for j in feed_forward(i):
                    ff_relu(j, 2)
                    ff_square(j, 2)
                for b in attention(i):
                    att_weight(b)
                for j in feed_forward(i):
                    ff_relu(j, 3)
                    ff_square(j, 3)
                for j in feed_forward(i + 1):
                    ff_hi(j)
                for b in attention(i + 1):
                    att_part_hi(b)

        @block.vector
        def _(dve):
            def layer_norm(kind, turn, source, affine):
                for t in range(NT):
                    nc.vector.bn_stats(stats[kind][:, t, :], source[:, t, :]).then_inc(stats_made[kind], 1)
                for t in range(NT):
                    dve.wait_ge(stats_made[kind], NT * turn + t + 1)
                    nc.vector.bn_aggr(moments[kind][:, t, :], stats[kind][:, t, :]).then_inc(moments_made[kind], 1)
                if turn:
                    dve.wait_ge(normed_made[kind], NT * turn)
                dve.wait_ge(moments_made[kind], NT * (turn + 1))
                nc.vector.tensor_scalar(var_eps[kind][:], moments[kind][:, :, 1], *affine, ALU.mult,
                                        ALU.add).then_inc(ln_args_made[kind], 1)
                nc.vector.tensor_scalar(neg_mean[kind][:], moments[kind][:, :, 0], -1.0, None,
                                        ALU.mult).then_inc(ln_args_made[kind], 1)

            def ff_layer_norm(j):
                if j.layer == "first":
                    dve.wait_ge(x_loaded[j.batch], 16)
                else:
                    dve.wait_ge(x_made["second"], j.batch + 1)
                layer_norm(j.lane, j.turn, x_of[j.layer][j.batch], FF_AFFINE)

            def att_layer_norm(b):
                dve.wait_ge(x_made["att"], b + 1)
                layer_norm("att", b, x_of["att"][b], ATT_AFFINE)

            def ff_lo(j):
                dve.wait_ge(hi_made[j.lane], j.turn + 1)
                nc.vector.tensor_tensor(in_lo[j.lane][:], work[j.lane][:], in_hi[j.lane][:].bitcast(F32),
                                        ALU.subtract).then_inc(lo_made[j.lane], 1)

            def att_part_lo(b):
                dve.wait_ge(hi_made["att"], b + 1)
                nc.vector.tensor_tensor(att_lo[b % ATT_SETS][:], att_work[:], att_hi[b % ATT_SETS][:].bitcast(F32),
                                        ALU.subtract).then_inc(lo_made["att"], 1)

            def ff_sum_sign(j, k):
                if k <= j.sign_adds:
                    dve.wait_ge(signs_made[j.lane], NL * j.turn + k + 1)
                    so_far = signs[j.lane][:, 0, :]
                    if k > 1:
                        so_far = sign_sum[j.lane][:]
                        dve.wait_ge(sign_sum_made[j.lane], j.before(lambda other: other.sign_adds) + k - 1)
                    nc.vector.tensor_tensor(sign_sum[j.lane][:], so_far, signs[j.lane][:, k, :],
                                            ALU.add).then_inc(sign_sum_made[j.lane], 1)

            def ff_add(j):
                dve.wait_ge(count_made[j.lane], j.turn + 1)
                nc.vector.scalar_tensor_tensor(
                    flat(x_of[NEXT[j.layer]][j.batch]), count_bank[:], RESIDUAL_STEP / 2,
                    flat(x_of[j.layer][j.batch]), ALU.mult, ALU.add).then_inc(x_made[NEXT[j.layer]], 1)

            def att_sum(b):
                dve.wait_ge(weight_made, b + 1)
                nc.vector.tensor_tensor_scan(weight_sum[b % ATT_SETS][:], ones[:], weight[b % ATT_SETS][:], 0.0,
                                             ALU.mult, ALU.add).then_inc(sum_made, 1)

            def att_invert(b, half):
                cols = slice(half * HALF, (half + 1) * HALF)
                dve.wait_ge(sum_made, b + 1)
                if b and half == 0:
                    dve.wait_ge(share_made, 2 * b)
                nc.vector.reciprocal(inv_sum[:, cols], weight_sum[b % ATT_SETS][:, cols]).then_inc(inv_made, 1)

            def att_pool(b):
                dve.wait_ge(share_key_made, 2 * (b + 1))
                nc.vector.tensor_tensor_scan(pooled[:], ones[:], share_key[:], 0.0, ALU.mult, ALU.add).then_inc(pooled_made, 1)

            def att_product(b):
                dve.wait_ge(pooled_made, b + 1)
                dve.wait_ge(value_mm, b + 1)
                if b:
                    dve.wait_ge(attended_turned, b)
                nc.vector.scalar_tensor_tensor(attended[:], att_value[:], kv_bias[:, 1:2], pooled[:],
                                               ALU.add, ALU.mult).then_inc(attended_made, 1)

            def att_add(b):
                dve.wait_ge(attended_turned, b + 1)
                nc.vector.scalar_tensor_tensor(flat(x_of["second"][b]), att_value[:], 2 * OFFSET, flat(x_of["att"][b]),
                                               ALU.add, ALU.add).then_inc(x_made["second"], 1)

            def fc_low_part():
                dve.wait_ge(ident_made, 1)
                nc.vector.tensor_copy(ident16[:], ident[:]).then_inc(ident16_made, 1)
                dve.wait_ge(fc_hi_made, 1)
                nc.vector.tensor_tensor(flat(fc_lo), hidden[2][:], flat(fc_hi).bitcast(F32), ALU.subtract).then_inc(fc_ready, 1)

            nc.vector.memset(ones[:], 1.0).then_inc(consts_made, 1)
            def attention_weights():
                dve.wait_ge(att_turned, 1)
                nc.vector.tensor_copy(flat(att_t), att_work[:, 0:3 * P]).then_inc(att_copied, 1)
                dve.wait_ge(att_copied, 1)
                dve.wait_ge(vectors_loaded, 16 * 5)
                nc.vector.tensor_scalar(kv_full[:], att_t[:, 0:2, :], vectors[:, 3:4], None, ALU.mult).then_inc(kv_full_made, 1)
                dve.wait_ge(kv_full_made, 1)
                nc.vector.tensor_copy(kv_hi[:], kv_full[:]).then_inc(kv_hi_made, 1)
                dve.wait_ge(kv_hi_made, 1)
                nc.vector.tensor_tensor(kv_lo[:], kv_full[:], kv_hi[:].bitcast(F32), ALU.subtract).then_inc(kv_ready, 1)

            def attention_biases():
                dve.wait_ge(beta_mm, 1)
                nc.vector.tensor_tensor(kv_bias[:], att_value[:, 0:2], vectors[:, 0:2], ALU.add).then_inc(bias_ready, 1)
                nc.vector.tensor_scalar(key_bias[:], vectors[:, 2:3], KEY_SCALE, None, ALU.mult).then_inc(bias_ready, 1)

            for i in range(FIRST_STEP, STEPS):
                for b in attention(i - 2):
                    att_invert(b, 0)
                for b in attention(i - 3):
                    att_add(b)
                for j in feed_forward(i - 2):
                    ff_sum_sign(j, 1)
                    ff_sum_sign(j, 2)
                for b in attention(i - 2):
                    att_invert(b, 1)
                for j in feed_forward(i - 2):
                    ff_sum_sign(j, 3)
                    ff_sum_sign(j, 4)
                for j in feed_forward(i + 1):
                    ff_layer_norm(j)
                for b in attention(i - 1):
                    att_sum(b)
                for j in feed_forward(i):
                    ff_lo(j)
                for b in attention(i - 2):
                    att_pool(b)
                for b in attention(i):
                    att_part_lo(b)
                for b in attention(i - 2):
                    att_product(b)
                for j in feed_forward(i - 2):
                    ff_add(j)
                for b in attention(i + 1):
                    att_layer_norm(b)
                if i == -1:
                    fc_low_part()
                if i == 0:
                    attention_weights()
                if i == 1:
                    attention_biases()

        @block.tensor
        def _(pe):
            def product(dst, w_hi, w_lo, x_hi, x_lo):
                nc.tensor.matmul(dst, w_lo, x_hi, start=True, stop=False)
                nc.tensor.matmul(dst, w_hi, x_lo, start=False, stop=False)
                return nc.tensor.matmul(dst, w_hi, x_hi, start=False, stop=True)

            def ff_turn(j):
                if j.turn:
                    pe.wait_ge(signs_made[j.lane], NL * j.turn)
                for t in range(NT):
                    pe.wait_ge(normed_made[j.lane], NT * j.turn + t + 1)
                    last = nc.tensor.transpose(work[j.lane][:, t * P:(t + 1) * P], normed[j.lane][:, t, :], ident[:])
                last.then_inc(turned[j.lane], 1)

            def ff_expand(j, c):
                if c == 0:
                    pe.wait_ge(lo_made[j.lane], j.turn + 1)
                for last in feed_forward(j.index - 1):
                    pe.wait_ge(relu_made[last.lane], NC * last.turn + c + 1)
                if hidden[c] is count_bank:
                    for last in feed_forward(j.index - 2):
                        pe.wait_ge(x_made[NEXT[last.layer]], last.batch + 1)
                product(hidden[c][:], fc_hi[:, c, :], fc_lo[:, c, :], in_hi[j.lane][:],
                        in_lo[j.lane][:]).then_inc(hidden_made[j.lane], 1)

            def ff_contract(j, c):
                if j.index == 0:
                    pe.wait_ge(proj_ready, 1)
                if c in j.act_squares:
                    pe.wait_ge(squares_act[j.lane], j.before(lambda k: len(k.act_squares)) + j.act_squares.index(c) + 1)
                else:
                    pe.wait_ge(squares_pool[j.lane], j.before(lambda k: len(k.pool_squares)) + j.pool_squares.index(c) + 1)
                mm = nc.tensor.matmul(work[j.lane][:], proj_t[:, c, :], square[j.lane][:, c, :],
                                      start=(c == CONTRACT_ORDER[0]), stop=(c == CONTRACT_ORDER[-1]))
                if c == CONTRACT_ORDER[-1]:
                    mm.then_inc(y_made[j.lane], 1)

            def ff_count(j):
                addends = [sign_sum[j.lane][:]] if j.sign_adds else [signs[j.lane][:, 0, :]]
                addends += [signs[j.lane][:, k, :] for k in range(j.sign_adds + 1, NL)]
                if j.sign_adds:
                    pe.wait_ge(sign_sum_made[j.lane], j.before(lambda other: other.sign_adds) + j.sign_adds)
                if j.sign_adds < NL - 1:
                    pe.wait_ge(signs_made[j.lane], NL * (j.turn + 1))
                for last in (feed_forward(j.index + 1) or feed_forward(len(FF_JOBS) - 1)):
                    pe.wait_ge(relu_made[last.lane], NC * (last.turn + 1))
                for t in range(NT):
                    tokens = slice(t * P, (t + 1) * P)
                    for k, addend in enumerate(addends):
                        last = nc.tensor.matmul(count_bank[:, tokens], addend[:, tokens], ident16[:],
                                                start=(k == 0), stop=(k == len(addends) - 1))
                last.then_inc(count_made[j.lane], 1)

            def att_turn(b):
                if b:
                    pe.wait_ge(weight_made, b)
                for t in range(NT):
                    pe.wait_ge(normed_made["att"], NT * b + t + 1)
                    last = nc.tensor.transpose(att_work[:, t * P:(t + 1) * P], normed["att"][:, t, :], ident[:])
                last.then_inc(turned["att"], 1)

            def att_keys(b):
                pe.wait_ge(lo_made["att"], b + 1)
                product(att_work[:], kv_hi[:, 0, :], kv_lo[:, 0, :], att_hi[b % ATT_SETS][:], att_lo[b % ATT_SETS][:]).then_inc(key_mm, 1)

            def att_values(b):
                if b:
                    pe.wait_ge(x_made["second"], b)
                product(att_value[:], kv_hi[:, 1, :], kv_lo[:, 1, :], att_hi[b % ATT_SETS][:], att_lo[b % ATT_SETS][:]).then_inc(value_mm, 1)

            def att_key_attention(b):
                pe.wait_ge(key_made, b + 1)
                nc.tensor.matmul(att_work[:], att_t[:, 2, :], key[b % ATT_SETS][:], start=True, stop=True).then_inc(att_mm, 1)

            def att_turn_back(b):
                pe.wait_ge(attended_made, b + 1)
                for t in range(NT):
                    last = nc.tensor.transpose(att_value[:, t * P:(t + 1) * P], attended[:, t * P:(t + 1) * P], ident[:])
                last.then_inc(attended_turned, 1)

            pe.wait_ge(ident_made, 1)
            for _ in range(WARM_UP):
                nc.tensor.transpose(hidden[0][:, 0:P], ident[:], ident[:])
            pe.wait_ge(fc_loaded, 16)
            for c in range(NC):
                last = nc.tensor.transpose(hidden[2][:, c * P:(c + 1) * P], fc_raw[:, c, :], ident[:])
            last.then_inc(fc_turned, 1)
            pe.wait_ge(proj_loaded, 16)
            for c in range(NC):
                last = nc.tensor.transpose(att_value[:, c * P:(c + 1) * P], proj_raw[:, c, :], ident[:])
            last.then_inc(proj_turned, 1)
            for i in range(FIRST_STEP, STEPS):
                for b in attention(i - 3):
                    att_turn_back(b)
                for j in feed_forward(i - 1):
                    ff_expand(j, 3)
                    ff_contract(j, 1)
                for b in attention(i - 1):
                    att_key_attention(b)
                for j in feed_forward(i - 1):
                    ff_contract(j, 0)
                for j in feed_forward(i):
                    ff_turn(j)
                for j in feed_forward(i - 1):
                    ff_contract(j, 2)
                for b in attention(i):
                    att_turn(b)
                for b in attention(i - 2):
                    att_values(b)
                for j in feed_forward(i - 1):
                    ff_contract(j, 3)
                for j in feed_forward(i - 2):
                    ff_count(j)
                if i == 0:
                    for _ in range(WARM_UP):
                        nc.tensor.transpose(hidden[0][:, 0:P], ident[:], ident[:])
                    pe.wait_ge(fc_ready, 1)
                for j in feed_forward(i):
                    ff_expand(j, 0)
                    ff_expand(j, 1)
                    ff_expand(j, 2)
                for b in attention(i):
                    att_keys(b)
                if i == 0:
                    pe.wait_ge(att_loaded, 16 * 3)
                    for a in range(3):
                        last = nc.tensor.transpose(att_work[:, a * P:(a + 1) * P], att_raw[:, a, :], ident[:])
                    last.then_inc(att_turned, 1)
                if i == 1:
                    pe.wait_ge(att_copied, 1)
                    pe.wait_ge(vectors_loaded, 16 * 5)
                    for a in range(2):
                        last = nc.tensor.matmul(att_value[:, a:a + 1], att_t[:, a, :], vectors[:, 4:5], start=True, stop=True)
                    last.then_inc(beta_mm, 1)
                    pe.wait_ge(kv_ready, 1)
                    pe.wait_ge(ident16_made, 1)
                    pe.wait_ge(bias_ready, 2)


_INS = ["L0_attn_hidden_states", "L0_attn_Wk", "L0_attn_bk", "L0_attn_Wka", "L0_attn_bka", "L0_attn_Wv",
        "L0_attn_bv", "L0_attn_gamma", "L0_attn_beta", "L0_ffn_W_fc", "L0_ffn_W_proj"]


def kernel(**inputs):
    import numpy as _np
    import concourse.bacc as _bacc
    from concourse import mybir as _mybir
    from concourse.bass_utils import run_bass_kernel_spmd as _run

    nc = _bacc.Bacc("TRN2", target_bir_lowering=False, num_devices=1)
    arrays, args = {}, []
    for name in _INS:
        a = _np.ascontiguousarray(inputs[name])
        arrays[f"in_{name}_dram"] = a
        args.append(nc.dram_tensor(f"in_{name}_dram", a.shape, _mybir.dt.from_np(a.dtype), kind="ExternalInput").ap())
    shape = inputs["L0_attn_hidden_states"].shape
    out = nc.dram_tensor("out_0_dram", shape, _mybir.dt.float32, kind="ExternalOutput").ap()
    macaron_kernel(nc, *args, out)
    r = _run(nc, [arrays], core_ids=[0])
    return r.results[0]["out_0_dram"]
```

```python
from contextlib import ExitStack

import numpy as np

import concourse.bass as bass
from concourse import mybir

P = 128
F32 = mybir.dt.float32
F32R = mybir.dt.float32r
BF16 = mybir.dt.bfloat16
ALU = mybir.AluOpType
ACT = mybir.ActivationFunctionType

LN_EPS = 1e-5
SPIKE_DECAY, SPIKE_THRESHOLD, SPIKE_STEPS = 0.9, 1.0, 5


FF_JOBS = [("first", b) for b in range(7)] + \
          [("second", 0)] + \
          [("first", 7)] + \
          [("second", b) for b in range(1, 8)]
ATT_STEP = [3, 4, 5, 7, 8, 9, 10, 11]
CONTRACT_ORDER = (0, 1, 2, 3)
DVE_SQUARES = [(0,), ()]
LAST_DVE_SQUARES = (1,)
POOL_SQUARES = [(0,), (0,)]
SIGN_ADDS = [4, 0]
LAST_SIGN_ADDS = 3
ATT_SETS = 3


class FeedForward:

    def __init__(self, i):
        self.layer, self.batch = FF_JOBS[i]
        self.index, self.lane, self.turn = i, i % 2, i // 2
        self.dve_squares = DVE_SQUARES[i in ATT_STEP] if i < len(FF_JOBS) - 2 else LAST_DVE_SQUARES
        self.pool_squares = [c for c in POOL_SQUARES[i in ATT_STEP] if c not in self.dve_squares]
        self.act_squares = [c for c in CONTRACT_ORDER if c not in self.dve_squares and c not in self.pool_squares]
        self.sign_adds = LAST_SIGN_ADDS if i == len(FF_JOBS) - 1 else SIGN_ADDS[i in ATT_STEP]

    def before(self, amount):
        return sum(amount(FeedForward(k)) for k in range(self.lane, self.index, 2))


def feed_forward(i):
    return [FeedForward(i)] if 0 <= i < len(FF_JOBS) else []


def attention(i):
    return [ATT_STEP.index(i)] if i in ATT_STEP else []


def spike_count(y):
    one = np.float32(SPIKE_THRESHOLD)
    mem, count = np.float32(0), 0
    for _ in range(SPIKE_STEPS):
        reset = np.float32(mem - one > 0)
        mem = np.float32(np.float32(np.float32(SPIKE_DECAY) * mem) + y) - reset * one
        count += int(mem - one > 0)
    return count


def spike_levels():
    levels = []
    for k in range(1, SPIKE_STEPS + 1):
        low, high = (int(np.float32(v).view(np.uint32)) for v in (0.1, 2.0))
        while high - low > 1:
            mid = (low + high) // 2
            if spike_count(np.uint32(mid).view(np.float32)) >= k:
                high = mid
            else:
                low = mid
        levels.append(np.uint32(low).view(np.float32))
    return levels


def sign_form(level):
    ulp = 2.0 ** (int(np.floor(np.log2(level))) - 23)
    middle2 = 2 * int(float(level) / ulp) + 1
    for k in range(1, 4096):
        scale = 2**23 + k
        product = scale * middle2
        bias = float(np.float32(product * ulp * 2.0**-24))
        off = abs(int(bias / ulp * 2.0**24) - product)
        if off < 2**21:
            return scale * 2.0**-23, -bias
    raise ValueError("no scale separates the two")


def macaron_kernel(nc, x, wk, bk, wka, bka, wv, bv, gamma, beta, w_fc, w_proj, out):
    NB, S, D = x.shape
    NT = S // P
    FF = w_fc.shape[0]
    NC = FF // P
    HALF = S // 2
    assert D == P and S == 512 and FF == 512
    assert sorted(FF_JOBS) == sorted((l, b) for l in ("first", "second") for b in range(NB))
    for b in range(NB):
        assert FF_JOBS.index(("first", b)) + 3 <= ATT_STEP[b] <= FF_JOBS.index(("second", b)) - 3
    KEY_SCALE = float(1.0 / np.sqrt(np.float32(D)))
    LEVELS = [sign_form(level) for level in spike_levels()]
    NL = len(LEVELS)
    RESIDUAL_STEP = 0.5 / SPIKE_STEPS
    OFFSET = NL * RESIDUAL_STEP / 2
    WARM_UP = 14
    STEPS = len(FF_JOBS) + 3
    FIRST_STEP = -3
    FF_AFFINE, ATT_AFFINE = (1.0, LN_EPS), (1.0 + LN_EPS, LN_EPS * LN_EPS)

    with ExitStack() as ctx:
        def sb(name, shape, dtype=F32):
            return ctx.enter_context(nc.sbuf_tensor(name, shape, dtype))

        def sem(name):
            return ctx.enter_context(nc.semaphore(name))

        def bank(name):
            return ctx.enter_context(nc.psum_tensor(name, [P, 512], F32))

        LANES = (0, 1)
        KINDS = (0, 1, "att")

        hidden = [bank(f"hidden{c}") for c in range(NC)]
        count_bank = hidden[NC - 1]
        work = [bank(f"work{l}") for l in LANES]
        att_work, att_value = bank("att_work"), bank("att_value")

        ident = sb("ident", [P, P])
        ident16 = sb("ident16", [P, P], BF16)
        ones = sb("ones", [P, S])
        minus_half = sb("minus_half", [P, NT])
        fc_raw = sb("fc_raw", [P, NC, P])
        proj_raw = sb("proj_raw", [P, NC, P])
        att_raw = sb("att_raw", [P, 3, P])
        vectors = sb("vectors", [P, 5])
        fc_hi = sb("fc_hi", [P, NC, P], F32R)
        fc_lo = sb("fc_lo", [P, NC, P], F32R)
        proj_t = sb("proj_t", [P, NC, P])
        att_t = sb("att_t", [P, 3, P])
        att_w = sb("att_w", [P, 3, P])
        att_w_hi = sb("att_w_hi", [P, 3, P], F32R)
        att_w_lo = sb("att_w_lo", [P, 3, P], F32R)
        kv_bias = sb("kv_bias", [P, 2])
        exp_bias = sb("exp_bias", [P, 1])

        x_of = {k: [sb(f"x_{k}_{b}", [P, NT, P]) for b in range(NB)] for k in ("first", "att", "second", "out")}
        NEXT = {"first": "att", "second": "out"}

        stats = {k: sb(f"stats_{k}", [P, NT, 6]) for k in KINDS}
        moments = {k: sb(f"moments_{k}", [P, NT, 2]) for k in KINDS}
        neg_mean = {k: sb(f"neg_mean_{k}", [P, NT]) for k in KINDS}
        var_eps = {k: sb(f"var_eps_{k}", [P, NT]) for k in KINDS}
        rstd = {k: sb(f"rstd_{k}", [P, NT]) for k in KINDS}
        normed = {k: sb(f"normed_{k}", [P, NT, P]) for k in KINDS}
        in_hi = [sb(f"in_hi{l}", [P, S], F32R) for l in LANES]
        in_lo = [sb(f"in_lo{l}", [P, S], F32R) for l in LANES]
        relu = [sb(f"relu{l}", [P, NC, S]) for l in LANES]
        square = [sb(f"square{l}", [P, NC, S]) for l in LANES]
        signs = [sb(f"signs{l}", [P, NL, S], BF16) for l in LANES]
        sign_sum = [sb(f"sign_sum{l}", [P, S], BF16) for l in LANES]
        att_hi = [sb(f"att_hi{k}", [P, S], F32R) for k in range(ATT_SETS)]
        att_lo = [sb(f"att_lo{k}", [P, S], F32R) for k in range(ATT_SETS)]
        key = [sb(f"key{k}", [P, S]) for k in range(ATT_SETS)]
        weight = [sb(f"weight{k}", [P, S]) for k in range(ATT_SETS)]
        weight_sum = [sb(f"weight_sum{k}", [P, S]) for k in range(ATT_SETS)]
        inv_sum = sb("inv_sum", [P, S])
        share = sb("share", [P, S])
        share_key = sb("share_key", [P, S])
        pooled = sb("pooled", [P, S])
        attended = sb("attended", [P, S])

        zeros_made, ident_made, ident16_made = sem("zeros_made"), sem("ident_made"), sem("ident16_made")
        consts_made = sem("consts_made")
        x_loaded = [sem(f"x_loaded{b}") for b in range(NB)]
        fc_loaded, proj_loaded, att_loaded = sem("fc_loaded"), sem("proj_loaded"), sem("att_loaded")
        vectors_loaded = sem("vectors_loaded")
        fc_turned, proj_turned, att_turned = sem("fc_turned"), sem("proj_turned"), sem("att_turned")
        beta_mm = sem("beta_mm")
        fc_hi_made, fc_ready, proj_ready = sem("fc_hi_made"), sem("fc_ready"), sem("proj_ready")
        att_copied, fold_mm, att_w_made = sem("att_copied"), sem("fold_mm"), sem("att_w_made")
        att_w_hi_made, att_w_ready = sem("att_w_hi_made"), sem("att_w_ready")
        kv_bias_made, exp_bias_mm, exp_bias_made = sem("kv_bias_made"), sem("exp_bias_mm"), sem("exp_bias_made")
        out_stored = sem("out_stored")

        def sems(name, kinds):
            return {k: sem(f"{name}_{k}") for k in kinds}

        stats_made, moments_made = sems("stats_made", KINDS), sems("moments_made", KINDS)
        ln_args_made, rstd_made = sems("ln_args_made", KINDS), sems("rstd_made", KINDS)
        normed_made = sems("normed_made", KINDS)
        turned, hi_made, lo_made = sems("turned", KINDS), sems("hi_made", KINDS), sems("lo_made", KINDS)
        hidden_made, relu_made = sems("hidden_made", LANES), sems("relu_made", LANES)
        squares_act, squares_pool = sems("squares_act", LANES), sems("squares_pool", LANES)
        squares_dve = sems("squares_dve", LANES)
        y_made, count_made = sems("y_made", LANES), sems("count_made", LANES)
        signs_made = sems("signs_made", LANES)
        sign_sum_made = sems("sign_sum_made", LANES)
        x_made = sems("x_made", ("att", "second", "out"))
        key_mm, value_mm, key_made, att_mm = sem("key_mm"), sem("value_mm"), sem("key_made"), sem("att_mm")
        weight_made, sum_made, inv_made = sem("weight_made"), sem("sum_made"), sem("inv_made")
        share_made, share_key_made = sem("share_made"), sem("share_key_made")
        pooled_made, attended_made, attended_turned = sem("pooled_made"), sem("attended_made"), sem("attended_turned")

        def flat(tile):
            return tile[:].rearrange("p t d -> p (t d)")

        def wait_relu(engine, j, c):
            engine.wait_ge(relu_made[j.lane], NC * j.turn + c + 1)

        def wait_dve_square(engine, j, c):
            engine.wait_ge(squares_dve[j.lane], j.before(lambda k: len(k.dve_squares)) + j.dve_squares.index(c) + 1)

        x_tiles = x.rearrange("b (t p) d -> b p t d", p=P)
        out_tiles = out.rearrange("b (t p) d -> b p t d", p=P)
        block = ctx.enter_context(nc.Block())

        @block.sync
        def _(sp):
            sp.dma_start(x_of["first"][0][:], x_tiles[0]).then_inc(x_loaded[0], 16)
            sp.dma_start(proj_raw[:], w_proj.rearrange("d (c f) -> d c f", f=P)).then_inc(proj_loaded, 16)
            sp.dma_start(x_of["first"][1][:], x_tiles[1]).then_inc(x_loaded[1], 16)
            for k, w in enumerate((wk, wv, wka)):
                sp.dma_start(att_raw[:, k, :], w).then_inc(att_loaded, 16)
            sp.dma_start(x_of["first"][2][:], x_tiles[2]).then_inc(x_loaded[2], 16)
            for k, v in enumerate((bk, bv, bka, gamma, beta)):
                sp.dma_start(vectors[:, k:k + 1], v.rearrange("(p a) -> p a", a=1)).then_inc(vectors_loaded, 16)
            for b in range(3, NB):
                sp.dma_start(x_of["first"][b][:], x_tiles[b]).then_inc(x_loaded[b], 16)
            for b in range(NB):
                sp.wait_ge(x_made["out"], b + 1)
                sp.dma_start(out_tiles[b], x_of["out"][b][:]).then_inc(out_stored, 16)
            sp.wait_ge(out_stored, 16 * NB)

        @block.gpsimd
        def _(pool):
            nc.gpsimd.memset(ident[:], 0.0).then_inc(zeros_made, 1)
            nc.gpsimd.memset(minus_half[:], -0.5).then_inc(zeros_made, 1)
            pool.wait_ge(zeros_made, 2)
            nc.gpsimd.affine_select(out=ident[:], in_=ident[:], compare_op=ALU.not_equal, fill=1.0,
                                    base=0, pattern=[[-1, P]], channel_multiplier=1).then_inc(ident_made, 1)

            def normalise(kind, turn, source):
                pool.wait_ge(ln_args_made[kind], 2 * (turn + 1))
                nc.gpsimd.tensor_tensor(rstd[kind][:], var_eps[kind][:], minus_half[:],
                                        ALU.pow).then_inc(rstd_made[kind], 1)
                pool.wait_ge(rstd_made[kind], turn + 1)
                if turn:
                    pool.wait_ge(turned[kind], turn)
                for t in range(NT):
                    nc.gpsimd.tensor_scalar(normed[kind][:, t, :], source[:, t, :], neg_mean[kind][:, t:t + 1],
                                            rstd[kind][:, t:t + 1], ALU.add, ALU.mult).then_inc(normed_made[kind], 1)

            def ff_normalise(j):
                normalise(j.lane, j.turn, x_of[j.layer][j.batch])

            def att_normalise(b):
                normalise("att", b, x_of["att"][b])

            def ff_squares(j):
                for c in j.pool_squares:
                    wait_relu(pool, j, c)
                    nc.gpsimd.tensor_tensor(square[j.lane][:, c, :], relu[j.lane][:, c, :], relu[j.lane][:, c, :],
                                            ALU.mult).then_inc(squares_pool[j.lane], 1)

            def att_shares(b, half):
                cols = slice(half * HALF, (half + 1) * HALF)
                pool.wait_ge(inv_made, 2 * b + half + 1)
                if half == 0:
                    pool.wait_ge(key_made, b + 1)
                if b and half == 0:
                    pool.wait_ge(pooled_made, b)
                nc.gpsimd.tensor_tensor(share[:, cols], weight[b % ATT_SETS][:, cols], inv_sum[:, cols],
                                        ALU.mult).then_inc(share_made, 1)
                pool.wait_ge(share_made, 2 * b + half + 1)
                nc.gpsimd.tensor_tensor(share_key[:, cols], share[:, cols], key[b % ATT_SETS][:, cols],
                                        ALU.mult).then_inc(share_key_made, 1)

            for i in range(FIRST_STEP, STEPS):
                for b in attention(i - 1):
                    att_shares(b, 0)
                    att_shares(b, 1)
                for j in feed_forward(i + 2):
                    ff_normalise(j)
                for j in feed_forward(i + 1):
                    ff_squares(j)
                for b in attention(i + 2):
                    att_normalise(b)

        @block.scalar
        def _(act):
            act.dma_start(fc_raw[:], w_fc.rearrange("(c p) d -> p c d", p=P)).then_inc(fc_loaded, 16)

            def ff_hi(j):
                act.wait_ge(turned[j.lane], j.turn + 1)
                nc.scalar.activation(in_hi[j.lane][:], work[j.lane][:], ACT.Copy).then_inc(hi_made[j.lane], 1)

            def ff_relu(j, c):
                act.wait_ge(hidden_made[j.lane], NC * j.turn + c + 1)
                nc.scalar.activation(relu[j.lane][:, c, :], hidden[c][:], ACT.Relu).then_inc(relu_made[j.lane], 1)

            def ff_square(j, c):
                if c in j.act_squares:
                    wait_relu(act, j, c)
                    nc.scalar.activation(square[j.lane][:, c, :], relu[j.lane][:, c, :],
                                         ACT.Square).then_inc(squares_act[j.lane], 1)

            def ff_sign(j, k):
                if k == 0:
                    act.wait_ge(y_made[j.lane], j.turn + 1)
                if k == 0 and j.turn:
                    act.wait_ge(count_made[j.lane], j.turn)
                scale, bias = LEVELS[k]
                nc.scalar.activation(signs[j.lane][:, k, :], work[j.lane][:], ACT.Sign, bias=bias,
                                     scale=scale).then_inc(signs_made[j.lane], 1)

            def att_part_hi(b):
                act.wait_ge(turned["att"], b + 1)
                if b >= ATT_SETS:
                    act.wait_ge(value_mm, b - ATT_SETS + 1)
                nc.scalar.activation(att_hi[b % ATT_SETS][:], att_work[:], ACT.Copy).then_inc(hi_made["att"], 1)

            def att_key(b):
                act.wait_ge(key_mm, b + 1)
                if b == 0:
                    act.wait_ge(kv_bias_made, 1)
                if b >= ATT_SETS:
                    act.wait_ge(share_key_made, 2 * (b - ATT_SETS + 1))
                nc.scalar.activation(key[b % ATT_SETS][:], att_work[:], ACT.Identity,
                                     bias=kv_bias[:, 0:1]).then_inc(key_made, 1)

            def att_weight(b):
                act.wait_ge(att_mm, b + 1)
                if b == 0:
                    act.wait_ge(exp_bias_made, 1)
                nc.scalar.activation(weight[b % ATT_SETS][:], att_work[:], ACT.Exp, bias=exp_bias[:, 0:1],
                                     scale=KEY_SCALE).then_inc(weight_made, 1)

            act.wait_ge(fc_turned, 1)
            nc.scalar.activation(flat(fc_hi), hidden[2][:], ACT.Copy).then_inc(fc_hi_made, 1)
            act.wait_ge(proj_turned, 1)
            nc.scalar.activation(flat(proj_t), att_value[:], ACT.Copy).then_inc(proj_ready, 1)
            for i in range(FIRST_STEP, STEPS):
                for j in feed_forward(i - 1):
                    ff_sign(j, 0)
                    ff_sign(j, 1)
                for j in feed_forward(i):
                    ff_relu(j, 0)
                for j in feed_forward(i - 1):
                    ff_sign(j, 2)
                    ff_sign(j, 3)
                for j in feed_forward(i):
                    ff_relu(j, 1)
                for j in feed_forward(i - 1):
                    ff_sign(j, 4)
                for b in attention(i):
                    att_weight(b)
                for j in feed_forward(i):
                    ff_square(j, 1)
                    ff_relu(j, 2)
                    ff_square(j, 2)
                    ff_relu(j, 3)
                for b in attention(i):
                    att_key(b)
                for j in feed_forward(i):
                    ff_square(j, 3)
                for j in feed_forward(i + 1):
                    ff_hi(j)
                for b in attention(i + 1):
                    att_part_hi(b)

        @block.vector
        def _(dve):
            def layer_norm(kind, turn, source, affine):
                for t in range(NT):
                    nc.vector.bn_stats(stats[kind][:, t, :], source[:, t, :]).then_inc(stats_made[kind], 1)
                for t in range(NT):
                    dve.wait_ge(stats_made[kind], NT * turn + t + 1)
                    nc.vector.bn_aggr(moments[kind][:, t, :], stats[kind][:, t, :]).then_inc(moments_made[kind], 1)
                if turn:
                    dve.wait_ge(normed_made[kind], NT * turn)
                dve.wait_ge(moments_made[kind], NT * (turn + 1))
                nc.vector.tensor_scalar(var_eps[kind][:], moments[kind][:, :, 1], *affine, ALU.mult,
                                        ALU.add).then_inc(ln_args_made[kind], 1)
                nc.vector.tensor_scalar(neg_mean[kind][:], moments[kind][:, :, 0], -1.0, None,
                                        ALU.mult).then_inc(ln_args_made[kind], 1)

            def ff_layer_norm(j):
                if j.layer == "first":
                    dve.wait_ge(x_loaded[j.batch], 16)
                else:
                    dve.wait_ge(x_made["second"], j.batch + 1)
                layer_norm(j.lane, j.turn, x_of[j.layer][j.batch], FF_AFFINE)

            def att_layer_norm(b):
                dve.wait_ge(x_made["att"], b + 1)
                layer_norm("att", b, x_of["att"][b], ATT_AFFINE)

            def ff_lo(j):
                dve.wait_ge(hi_made[j.lane], j.turn + 1)
                nc.vector.tensor_tensor(in_lo[j.lane][:], work[j.lane][:], in_hi[j.lane][:].bitcast(F32),
                                        ALU.subtract).then_inc(lo_made[j.lane], 1)

            def att_part_lo(b):
                dve.wait_ge(hi_made["att"], b + 1)
                nc.vector.tensor_tensor(att_lo[b % ATT_SETS][:], att_work[:], att_hi[b % ATT_SETS][:].bitcast(F32),
                                        ALU.subtract).then_inc(lo_made["att"], 1)

            def ff_dve_square(j, n):
                if n < len(j.dve_squares):
                    c = j.dve_squares[n]
                    wait_relu(dve, j, c)
                    nc.vector.tensor_tensor(square[j.lane][:, c, :], relu[j.lane][:, c, :], relu[j.lane][:, c, :],
                                            ALU.mult).then_inc(squares_dve[j.lane], 1)

            def ff_sum_sign(j, k):
                if k <= j.sign_adds:
                    dve.wait_ge(signs_made[j.lane], NL * j.turn + k + 1)
                    so_far = signs[j.lane][:, 0, :]
                    if k > 1:
                        so_far = sign_sum[j.lane][:]
                        dve.wait_ge(sign_sum_made[j.lane], j.before(lambda other: other.sign_adds) + k - 1)
                    nc.vector.tensor_tensor(sign_sum[j.lane][:], so_far, signs[j.lane][:, k, :],
                                            ALU.add).then_inc(sign_sum_made[j.lane], 1)

            def ff_add(j):
                dve.wait_ge(count_made[j.lane], j.turn + 1)
                nc.vector.scalar_tensor_tensor(
                    flat(x_of[NEXT[j.layer]][j.batch]), count_bank[:], RESIDUAL_STEP / 2,
                    flat(x_of[j.layer][j.batch]), ALU.mult, ALU.add).then_inc(x_made[NEXT[j.layer]], 1)

            def att_sum(b):
                dve.wait_ge(weight_made, b + 1)
                nc.vector.tensor_tensor_scan(weight_sum[b % ATT_SETS][:], ones[:], weight[b % ATT_SETS][:], 0.0,
                                             ALU.mult, ALU.add).then_inc(sum_made, 1)

            def att_invert(b, half):
                cols = slice(half * HALF, (half + 1) * HALF)
                dve.wait_ge(sum_made, b + 1)
                if b and half == 0:
                    dve.wait_ge(share_made, 2 * b)
                nc.vector.reciprocal(inv_sum[:, cols], weight_sum[b % ATT_SETS][:, cols]).then_inc(inv_made, 1)

            def att_pool(b):
                dve.wait_ge(share_key_made, 2 * (b + 1))
                nc.vector.tensor_tensor_scan(pooled[:], ones[:], share_key[:], 0.0, ALU.mult,
                                             ALU.add).then_inc(pooled_made, 1)

            def att_product(b):
                dve.wait_ge(pooled_made, b + 1)
                dve.wait_ge(value_mm, b + 1)
                if b:
                    dve.wait_ge(attended_turned, b)
                nc.vector.scalar_tensor_tensor(attended[:], att_value[:], kv_bias[:, 1:2], pooled[:],
                                               ALU.add, ALU.mult).then_inc(attended_made, 1)

            def att_add(b):
                dve.wait_ge(attended_turned, b + 1)
                nc.vector.scalar_tensor_tensor(flat(x_of["second"][b]), att_value[:], 2 * OFFSET, flat(x_of["att"][b]),
                                               ALU.add, ALU.add).then_inc(x_made["second"], 1)

            def fc_low_part():
                dve.wait_ge(ident_made, 1)
                nc.vector.tensor_copy(ident16[:], ident[:]).then_inc(ident16_made, 1)
                dve.wait_ge(fc_hi_made, 1)
                nc.vector.tensor_tensor(flat(fc_lo), hidden[2][:], flat(fc_hi).bitcast(F32),
                                        ALU.subtract).then_inc(fc_ready, 1)

            def attention_weights():
                dve.wait_ge(att_turned, 1)
                nc.vector.tensor_copy(flat(att_t), att_work[:, 0:3 * P]).then_inc(att_copied, 1)
                dve.wait_ge(att_copied, 1)
                dve.wait_ge(vectors_loaded, 16 * 5)
                nc.vector.tensor_scalar(att_w[:, 0:2, :], att_t[:, 0:2, :], vectors[:, 3:4], None,
                                        ALU.mult).then_inc(att_w_made, 1)

            def attention_folded():
                dve.wait_ge(fold_mm, 1)
                dve.wait_ge(beta_mm, 1)
                nc.vector.tensor_scalar(att_w[:, 2, :], att_value[:, P:2 * P], vectors[:, 3:4], None,
                                        ALU.mult).then_inc(att_w_made, 1)
                dve.wait_ge(att_w_made, 2)
                nc.vector.tensor_copy(att_w_hi[:], att_w[:]).then_inc(att_w_hi_made, 1)
                dve.wait_ge(att_w_hi_made, 1)
                nc.vector.tensor_tensor(att_w_lo[:], att_w[:], att_w_hi[:].bitcast(F32),
                                        ALU.subtract).then_inc(att_w_ready, 1)
                nc.vector.tensor_tensor(kv_bias[:], att_value[:, 0:2], vectors[:, 0:2], ALU.add).then_inc(kv_bias_made, 1)

            def attention_exp_bias():
                dve.wait_ge(exp_bias_mm, 1)
                nc.vector.tensor_scalar(exp_bias[:], att_value[:, 2:3], vectors[:, 2:3], KEY_SCALE, ALU.add,
                                        ALU.mult).then_inc(exp_bias_made, 1)

            nc.vector.memset(ones[:], 1.0).then_inc(consts_made, 1)
            for i in range(FIRST_STEP, STEPS):
                for j in feed_forward(i - 2):
                    ff_sum_sign(j, 1)
                for b in attention(i - 2):
                    att_invert(b, 0)
                for b in attention(i - 3):
                    att_add(b)
                for j in feed_forward(i - 2):
                    ff_sum_sign(j, 2)
                for j in feed_forward(i - 1):
                    ff_dve_square(j, 1)
                for b in attention(i - 2):
                    att_invert(b, 1)
                for j in feed_forward(i - 2):
                    ff_sum_sign(j, 3)
                    ff_sum_sign(j, 4)
                for j in feed_forward(i + 1):
                    ff_layer_norm(j)
                for b in attention(i - 1):
                    att_sum(b)
                for j in feed_forward(i):
                    ff_lo(j)
                for b in attention(i - 2):
                    att_pool(b)
                    att_product(b)
                for j in feed_forward(i - 2):
                    ff_add(j)
                for b in attention(i):
                    att_part_lo(b)
                for b in attention(i + 1):
                    att_layer_norm(b)
                for j in feed_forward(i):
                    ff_dve_square(j, 0)
                if i == -1:
                    fc_low_part()
                if i == 0:
                    attention_weights()
                if i == 1:
                    attention_folded()
                if i == 2:
                    attention_exp_bias()

        @block.tensor
        def _(pe):
            def product(dst, w_hi, w_lo, x_hi, x_lo):
                nc.tensor.matmul(dst, w_lo, x_hi, start=True, stop=False)
                nc.tensor.matmul(dst, w_hi, x_lo, start=False, stop=False)
                return nc.tensor.matmul(dst, w_hi, x_hi, start=False, stop=True)

            def ff_turn(j):
                if j.turn:
                    pe.wait_ge(signs_made[j.lane], NL * j.turn)
                for t in range(NT):
                    pe.wait_ge(normed_made[j.lane], NT * j.turn + t + 1)
                    last = nc.tensor.transpose(work[j.lane][:, t * P:(t + 1) * P], normed[j.lane][:, t, :], ident[:])
                last.then_inc(turned[j.lane], 1)

            def ff_expand(j, c):
                if c == 0:
                    pe.wait_ge(lo_made[j.lane], j.turn + 1)
                for last in feed_forward(j.index - 1):
                    wait_relu(pe, last, c)
                if hidden[c] is count_bank:
                    for last in feed_forward(j.index - 2):
                        pe.wait_ge(x_made[NEXT[last.layer]], last.batch + 1)
                product(hidden[c][:], fc_hi[:, c, :], fc_lo[:, c, :], in_hi[j.lane][:],
                        in_lo[j.lane][:]).then_inc(hidden_made[j.lane], 1)

            def ff_contract(j, c):
                if j.index == 0:
                    pe.wait_ge(proj_ready, 1)
                if c in j.dve_squares:
                    wait_dve_square(pe, j, c)
                elif c in j.act_squares:
                    made = j.before(lambda k: len(k.act_squares)) + j.act_squares.index(c) + 1
                    pe.wait_ge(squares_act[j.lane], made)
                else:
                    made = j.before(lambda k: len(k.pool_squares)) + j.pool_squares.index(c) + 1
                    pe.wait_ge(squares_pool[j.lane], made)
                mm = nc.tensor.matmul(work[j.lane][:], proj_t[:, c, :], square[j.lane][:, c, :],
                                      start=(c == CONTRACT_ORDER[0]), stop=(c == CONTRACT_ORDER[-1]))
                if c == CONTRACT_ORDER[-1]:
                    mm.then_inc(y_made[j.lane], 1)

            def ff_count(j):
                addends = [sign_sum[j.lane][:]] if j.sign_adds else [signs[j.lane][:, 0, :]]
                addends += [signs[j.lane][:, k, :] for k in range(j.sign_adds + 1, NL)]
                if j.sign_adds:
                    pe.wait_ge(sign_sum_made[j.lane], j.before(lambda other: other.sign_adds) + j.sign_adds)
                if j.sign_adds < NL - 1:
                    pe.wait_ge(signs_made[j.lane], NL * (j.turn + 1))
                for last in feed_forward(j.index + 1) or [j]:
                    wait_relu(pe, last, NC - 1)
                for t in range(NT):
                    tokens = slice(t * P, (t + 1) * P)
                    for k, addend in enumerate(addends):
                        last = nc.tensor.matmul(count_bank[:, tokens], addend[:, tokens], ident16[:],
                                                start=(k == 0), stop=(k == len(addends) - 1))
                last.then_inc(count_made[j.lane], 1)

            def att_turn(b):
                if b:
                    pe.wait_ge(key_made, b)
                for t in range(NT):
                    pe.wait_ge(normed_made["att"], NT * b + t + 1)
                    last = nc.tensor.transpose(att_work[:, t * P:(t + 1) * P], normed["att"][:, t, :], ident[:])
                last.then_inc(turned["att"], 1)

            def att_mm_of(b, which, dst):
                return product(dst, att_w_hi[:, which, :], att_w_lo[:, which, :],
                               att_hi[b % ATT_SETS][:], att_lo[b % ATT_SETS][:])

            def att_key_attention(b):
                pe.wait_ge(lo_made["att"], b + 1)
                att_mm_of(b, 2, att_work[:]).then_inc(att_mm, 1)

            def att_keys(b):
                pe.wait_ge(weight_made, b + 1)
                att_mm_of(b, 0, att_work[:]).then_inc(key_mm, 1)

            def att_values(b):
                if b:
                    pe.wait_ge(x_made["second"], b)
                att_mm_of(b, 1, att_value[:]).then_inc(value_mm, 1)

            def att_turn_back(b):
                pe.wait_ge(attended_made, b + 1)
                for t in range(NT):
                    last = nc.tensor.transpose(att_value[:, t * P:(t + 1) * P], attended[:, t * P:(t + 1) * P], ident[:])
                last.then_inc(attended_turned, 1)

            pe.wait_ge(ident_made, 1)
            for _ in range(WARM_UP):
                nc.tensor.transpose(hidden[0][:, 0:P], ident[:], ident[:])
            pe.wait_ge(fc_loaded, 16)
            for c in range(NC):
                last = nc.tensor.transpose(hidden[2][:, c * P:(c + 1) * P], fc_raw[:, c, :], ident[:])
            last.then_inc(fc_turned, 1)
            pe.wait_ge(proj_loaded, 16)
            for c in range(NC):
                last = nc.tensor.transpose(att_value[:, c * P:(c + 1) * P], proj_raw[:, c, :], ident[:])
            last.then_inc(proj_turned, 1)
            for i in range(FIRST_STEP, STEPS):
                for b in attention(i - 3):
                    att_turn_back(b)
                for j in feed_forward(i - 1):
                    ff_expand(j, 2)
                for b in attention(i - 1):
                    att_key_attention(b)
                for j in feed_forward(i - 1):
                    ff_expand(j, 3)
                    ff_contract(j, 0)
                for b in attention(i - 1):
                    att_keys(b)
                for j in feed_forward(i):
                    ff_turn(j)
                for j in feed_forward(i - 1):
                    ff_contract(j, 1)
                    ff_contract(j, 2)
                for b in attention(i):
                    att_turn(b)
                for b in attention(i - 2):
                    att_values(b)
                for j in feed_forward(i - 1):
                    ff_contract(j, 3)
                for j in feed_forward(i - 2):
                    ff_count(j)
                if i == 0:
                    for _ in range(WARM_UP):
                        nc.tensor.transpose(hidden[0][:, 0:P], ident[:], ident[:])
                    pe.wait_ge(fc_ready, 1)
                for j in feed_forward(i):
                    ff_expand(j, 0)
                    ff_expand(j, 1)
                if i == 0:
                    pe.wait_ge(ident16_made, 1)
                    pe.wait_ge(att_loaded, 16 * 3)
                    for a in range(3):
                        last = nc.tensor.transpose(att_work[:, a * P:(a + 1) * P], att_raw[:, a, :], ident[:])
                    last.then_inc(att_turned, 1)
                if i == 1:
                    pe.wait_ge(att_copied, 1)
                    pe.wait_ge(vectors_loaded, 16 * 5)
                    nc.tensor.matmul(att_value[:, P:2 * P], att_raw[:, 0, :], att_t[:, 2, :], start=True,
                                     stop=True).then_inc(fold_mm, 1)
                    for a in range(2):
                        last = nc.tensor.matmul(att_value[:, a:a + 1], att_t[:, a, :], vectors[:, 4:5], start=True,
                                                stop=True)
                    last.then_inc(beta_mm, 1)
                if i == 2:
                    pe.wait_ge(kv_bias_made, 1)
                    nc.tensor.matmul(att_value[:, 2:3], att_t[:, 2, :], kv_bias[:, 0:1], start=True,
                                     stop=True).then_inc(exp_bias_mm, 1)


_INS = ["L0_attn_hidden_states", "L0_attn_Wk", "L0_attn_bk", "L0_attn_Wka", "L0_attn_bka", "L0_attn_Wv",
        "L0_attn_bv", "L0_attn_gamma", "L0_attn_beta", "L0_ffn_W_fc", "L0_ffn_W_proj"]


def kernel(**inputs):
    import numpy as _np
    import concourse.bacc as _bacc
    from concourse import mybir as _mybir
    from concourse.bass_utils import run_bass_kernel_spmd as _run

    nc = _bacc.Bacc("TRN2", target_bir_lowering=False, num_devices=1)
    arrays, args = {}, []
    for name in _INS:
        a = _np.ascontiguousarray(inputs[name])
        arrays[f"in_{name}_dram"] = a
        args.append(nc.dram_tensor(f"in_{name}_dram", a.shape, _mybir.dt.from_np(a.dtype), kind="ExternalInput").ap())
    shape = inputs["L0_attn_hidden_states"].shape
    out = nc.dram_tensor("out_0_dram", shape, _mybir.dt.float32, kind="ExternalOutput").ap()
    macaron_kernel(nc, *args, out)
    r = _run(nc, [arrays], core_ids=[0])
    return r.results[0]["out_0_dram"]
```
